# Optimizing a Trainium2 kernel written in Bass

```python
import numpy as np
import jax
import jax.numpy as jnp

def _softmax(x, axis=-1):
    return jax.nn.softmax(x, axis=axis)

def _gelu(x):
    return jax.nn.gelu(x, approximate=True)

def _silu(x):
    return jax.nn.silu(x)

def _sigmoid(x):
    return jax.nn.sigmoid(x)

def _layernorm(x, axis=-1, eps=1e-05):
    m = jnp.mean(x, axis=axis, keepdims=True)
    v = jnp.var(x, axis=axis, keepdims=True)
    return (x - m) / jnp.sqrt(v + eps)

def _scatter_add(tgt, idx, src, axis=0):
    return tgt.at[idx].add(src)

def _segment_sum(src, seg, n):
    return jax.ops.segment_sum(src, seg, n)
kernel_name = 'mk_flamingo_gated_d2_seqx_r4_70f2af'

def setup_inputs(seed: int=0):
    np.random.seed(seed)
    _w = jnp.asarray

    def _rec_inputs():
        import jax
        import jax.numpy as jnp
        _rk = jax.random.key(seed)
        x = -0.0002928 + 1 * jax.random.normal(jax.random.fold_in(_rk, 1), (4, 512, 256), jnp.float32)
        _lenS = 512 - jax.random.randint(jax.random.fold_in(_rk, 7), (4,), 0, max(1, 512 // 4) + 1, jnp.int32)
        _lenS2 = 64 - jax.random.randint(jax.random.fold_in(_rk, 8), (4,), 0, max(1, 64 // 4) + 1, jnp.int32)
        _ctx_1024P = jax.random.normal(jax.random.fold_in(_rk, 11), (4, 16, 256), jnp.float32)
        _ctx_1024c = jax.random.dirichlet(jax.random.fold_in(_rk, 511), 0.3 * jnp.ones((16,), jnp.float32), (4, 64))
        _ctx_1024t = jnp.einsum('bsk,bkd->bsd', _ctx_1024c, _ctx_1024P)
        _ctx_1024t = _ctx_1024t * jax.lax.rsqrt(jnp.mean(jnp.square(_ctx_1024t)) + 1e-12) * 0.953939
        ctx_1024 = -1.39393e-06 + 0.999914 * (_ctx_1024t + 0.3 * jax.random.normal(jax.random.fold_in(_rk, 611), (4, 64, 256), jnp.float32))
        _validS = jnp.arange(512)[None, :] < _lenS[:, None]
        _validS2 = jnp.arange(64)[None, :] < _lenS2[:, None]
        _causal = jnp.tril(jnp.ones((512, 512), dtype=bool))
        mask_1x1xSxS2_ik0 = jnp.where(jnp.broadcast_to(_validS2[0:1, None, None, :], (1, 1, 512, 64)), 0, 1).astype(jnp.int32)
        _g = jax.random.normal(jax.random.fold_in(_rk, 9001), (2, 2), jnp.float32)
        _g = jnp.sign(_g) * jnp.maximum(jnp.abs(_g), 1.0) + (_g == 0) * 1.0
        g_xattn = _g[0]
        g_ffn = _g[1]
        return (x, ctx_1024, mask_1x1xSxS2_ik0, g_xattn, g_ffn)
    x, ctx_1024, mask_1x1xSxS2_ik0, g_xattn, g_ffn = _rec_inputs()

    def _L0_xattn_setup():
        import jax, jax.numpy as jnp
        import numpy as np
        EMBED_DIM = 256
        NUM_HEADS = 16
        HEAD_DIM = EMBED_DIM // NUM_HEADS
        key = jax.random.key(seed)
        ks = jax.random.split(key, 7)
        B, S, E = (2, 512, EMBED_DIM)
        bound = float(np.sqrt(6.0 / (E + E)))
        mkw = lambda k: jax.random.uniform(k, (E, E), jnp.float32, -bound, bound)
        return {'query': jax.random.normal(ks[0], (B, S, E), jnp.float32), 'key': jax.random.normal(ks[1], (B, S, E), jnp.float32), 'value': jax.random.normal(ks[2], (B, S, E), jnp.float32), 'Wq': mkw(ks[3]), 'Wk': mkw(ks[4]), 'Wv': mkw(ks[5]), 'Wo': mkw(ks[6])}
    _L0_xattn_all = _L0_xattn_setup()
    _L0_xattn_in = {k: v for k, v in _L0_xattn_all.items() if k in ('Wq', 'Wk', 'Wv', 'Wo')}
    del _L0_xattn_all

    def _L0_ffn_setup():
        import jax, jax.numpy as jnp
        import numpy as np
        B, S, D, E = (4, 512, 256, 8)
        key = jax.random.key(seed)
        ks = jax.random.split(key, 5)
        s = 0.02
        return {'hidden_states': jax.random.normal(ks[0], (B, S, D), dtype=jnp.float32), 'Wr': jax.random.normal(ks[1], (D, E), dtype=jnp.float32) * s, 'br': jnp.zeros((E,), dtype=jnp.float32), 'W1': jax.random.normal(ks[2], (E, D, 4 * D), dtype=jnp.float32) * s, 'b1': jnp.zeros((E, 4 * D), dtype=jnp.float32), 'W2': jax.random.normal(ks[3], (E, 4 * D, 2 * D), dtype=jnp.float32) * s, 'b2': jnp.zeros((E, 2 * D), dtype=jnp.float32), 'W3': jax.random.normal(ks[4], (E, 2 * D, D), dtype=jnp.float32) * s, 'b3': jnp.zeros((E, D), dtype=jnp.float32)}
    _L0_ffn_all = _L0_ffn_setup()
    _L0_ffn_in = {k: v for k, v in _L0_ffn_all.items() if k in ('Wr', 'br', 'W1', 'b1', 'W2', 'b2', 'W3', 'b3')}
    del _L0_ffn_all

    def _L1_xattn_setup():
        import jax, jax.numpy as jnp
        import numpy as np
        B, T, D, H = (2, 512, 256, 16)
        DK = D // H
        key = jax.random.key(seed)
        ks = jax.random.split(key, 12)
        s = 1.0 / np.sqrt(D)
        inp = {'Q': jax.random.normal(ks[0], (B, T, D), jnp.float32), 'K': jax.random.normal(ks[1], (B, T, D), jnp.float32), 'V': jax.random.normal(ks[2], (B, T, D), jnp.float32), 'mask': jnp.tril(jnp.ones((T, T), jnp.int32))[None, None], 'Wq_w': jax.random.normal(ks[3], (D, D), jnp.float32) * s, 'Wq_b': jax.random.normal(ks[4], (D,), jnp.float32) * s, 'Wk_w': jax.random.normal(ks[5], (D, D), jnp.float32) * s, 'Wk_b': jax.random.normal(ks[6], (D,), jnp.float32) * s, 'Wv_w': jax.random.normal(ks[7], (D, D), jnp.float32) * s, 'Wv_b': jax.random.normal(ks[8], (D,), jnp.float32) * s, 'Wo_w': jax.random.normal(ks[9], (D, D), jnp.float32) * s, 'Wo_b': jax.random.normal(ks[10], (D,), jnp.float32) * s}
        return inp
    _L1_xattn_all = _L1_xattn_setup()
    _L1_xattn_in = {k: v for k, v in _L1_xattn_all.items() if k in ('Wq_w', 'Wq_b', 'Wk_w', 'Wk_b', 'Wv_w', 'Wv_b', 'Wo_w', 'Wo_b')}
    del _L1_xattn_all

    def _L1_ffn_setup():
        import jax, jax.numpy as jnp
        import numpy as np
        D_MODEL = 256
        HIDDEN = 1024
        N_ROUTING = 2
        key = jax.random.key(seed)
        ks = jax.random.split(key, 10)
        s = 0.02
        x = jax.random.normal(ks[0], (4, 1024, D_MODEL), dtype=jnp.float32)
        gate_w = jax.random.normal(ks[1], (N_ROUTING, D_MODEL), dtype=jnp.float32) * s
        w1 = jax.random.normal(ks[2], (N_ROUTING, D_MODEL, HIDDEN), dtype=jnp.float32) * s
        b1 = jax.random.normal(ks[3], (N_ROUTING, HIDDEN), dtype=jnp.float32) * s
        w2 = jax.random.normal(ks[4], (N_ROUTING, HIDDEN, D_MODEL), dtype=jnp.float32) * s
        b2 = jax.random.normal(ks[5], (N_ROUTING, D_MODEL), dtype=jnp.float32) * s
        sw1 = jax.random.normal(ks[6], (D_MODEL, HIDDEN), dtype=jnp.float32) * s
        sb1 = jax.random.normal(ks[7], (HIDDEN,), dtype=jnp.float32) * s
        sw2 = jax.random.normal(ks[8], (HIDDEN, D_MODEL), dtype=jnp.float32) * s
        sb2 = jax.random.normal(ks[9], (D_MODEL,), dtype=jnp.float32) * s
        return {'x': x, 'gate_w': gate_w, 'w1': w1, 'b1': b1, 'w2': w2, 'b2': b2, 'sw1': sw1, 'sb1': sb1, 'sw2': sw2, 'sb2': sb2}
    _L1_ffn_all = _L1_ffn_setup()
    _L1_ffn_in = {k: v for k, v in _L1_ffn_all.items() if k in ('gate_w', 'w1', 'b1', 'w2', 'b2', 'sw1', 'sb1', 'sw2', 'sb2')}
    del _L1_ffn_all
    return {'x': x, 'ctx_1024': ctx_1024, 'mask_1x1xSxS2_ik0': mask_1x1xSxS2_ik0, 'g_xattn': g_xattn, 'g_ffn': g_ffn, 'L0_xattn_Wq': _L0_xattn_in['Wq'], 'L0_xattn_Wk': _L0_xattn_in['Wk'], 'L0_xattn_Wv': _L0_xattn_in['Wv'], 'L0_xattn_Wo': _L0_xattn_in['Wo'], 'L0_ffn_Wr': _L0_ffn_in['Wr'], 'L0_ffn_br': _L0_ffn_in['br'], 'L0_ffn_W1': _L0_ffn_in['W1'], 'L0_ffn_b1': _L0_ffn_in['b1'], 'L0_ffn_W2': _L0_ffn_in['W2'], 'L0_ffn_b2': _L0_ffn_in['b2'], 'L0_ffn_W3': _L0_ffn_in['W3'], 'L0_ffn_b3': _L0_ffn_in['b3'], 'L1_xattn_Wq_w': _L1_xattn_in['Wq_w'], 'L1_xattn_Wq_b': _L1_xattn_in['Wq_b'], 'L1_xattn_Wk_w': _L1_xattn_in['Wk_w'], 'L1_xattn_Wk_b': _L1_xattn_in['Wk_b'], 'L1_xattn_Wv_w': _L1_xattn_in['Wv_w'], 'L1_xattn_Wv_b': _L1_xattn_in['Wv_b'], 'L1_xattn_Wo_w': _L1_xattn_in['Wo_w'], 'L1_xattn_Wo_b': _L1_xattn_in['Wo_b'], 'L1_ffn_gate_w': _L1_ffn_in['gate_w'], 'L1_ffn_w1': _L1_ffn_in['w1'], 'L1_ffn_b1': _L1_ffn_in['b1'], 'L1_ffn_w2': _L1_ffn_in['w2'], 'L1_ffn_b2': _L1_ffn_in['b2'], 'L1_ffn_sw1': _L1_ffn_in['sw1'], 'L1_ffn_sb1': _L1_ffn_in['sb1'], 'L1_ffn_sw2': _L1_ffn_in['sw2'], 'L1_ffn_sb2': _L1_ffn_in['sb2']}

def reference(x, ctx_1024, mask_1x1xSxS2_ik0, g_xattn, g_ffn, L0_xattn_Wq, L0_xattn_Wk, L0_xattn_Wv, L0_xattn_Wo, L0_ffn_Wr, L0_ffn_br, L0_ffn_W1, L0_ffn_b1, L0_ffn_W2, L0_ffn_b2, L0_ffn_W3, L0_ffn_b3, L1_xattn_Wq_w, L1_xattn_Wq_b, L1_xattn_Wk_w, L1_xattn_Wk_b, L1_xattn_Wv_w, L1_xattn_Wv_b, L1_xattn_Wo_w, L1_xattn_Wo_b, L1_ffn_gate_w, L1_ffn_w1, L1_ffn_b1, L1_ffn_w2, L1_ffn_b2, L1_ffn_sw1, L1_ffn_sb1, L1_ffn_sw2, L1_ffn_sb2):
    import jax
    import jax.numpy as jnp

    def _L0_xattn_ref(query, key, value, Wq, Wk, Wv, Wo):
        import jax, jax.numpy as jnp
        import numpy as np
        EMBED_DIM = 256
        NUM_HEADS = 16
        HEAD_DIM = EMBED_DIM // NUM_HEADS
        B, L, E = query.shape
        H, D = (NUM_HEADS, HEAD_DIM)
        scale = D ** (-0.5)
        q = (query @ Wq.T).reshape(B, L, H, D) * scale
        k = (key @ Wk.T).reshape(B, -1, H, D)
        v = (value @ Wv.T).reshape(B, -1, H, D)
        scores = jax.nn.sigmoid(jnp.einsum('blhd,bshd->bhls', q, k))
        o = jnp.einsum('bhls,bshd->blhd', scores, v).reshape(B, L, E)
        return o @ Wo.T

    def _L0_ffn_ref(hidden_states, Wr, br, W1, b1, W2, b2, W3, b3):
        import jax, jax.numpy as jnp
        import numpy as np
        B, S, D, E = (4, 512, 256, 8)
        b, s, d = hidden_states.shape
        num_experts = Wr.shape[1]
        x = hidden_states.reshape(-1, d)
        router_logits = x @ Wr + br
        expert_mask = jax.nn.one_hot(jnp.argmax(router_logits, axis=-1), num_experts, dtype=x.dtype)
        out = jnp.zeros_like(x)
        for e in range(num_experts):
            h = jax.nn.gelu(x @ W1[e] + b1[e], approximate=False)
            h = jax.nn.gelu(h @ W2[e] + b2[e], approximate=False)
            y = h @ W3[e] + b3[e]
            out = out + expert_mask[:, e:e + 1] * y
        return out.reshape(b, s, d)

    def _L1_xattn_ref(Q, K, V, mask, Wq_w, Wq_b, Wk_w, Wk_b, Wv_w, Wv_b, Wo_w, Wo_b):
        import jax, jax.numpy as jnp
        import numpy as np
        B, T, D, H = (2, 512, 256, 16)
        DK = D // H
        b, tq, c = Q.shape
        tk = K.shape[1]
        q = (Q @ Wq_w + Wq_b).reshape(b, tq, H, DK).transpose(0, 2, 1, 3)
        k = (K @ Wk_w + Wk_b).reshape(b, tk, H, DK).transpose(0, 2, 1, 3)
        v = (V @ Wv_w + Wv_b).reshape(b, tk, H, DK).transpose(0, 2, 1, 3)
        scores = jnp.einsum('bhqd,bhkd->bhqk', q, k) / jnp.sqrt(jnp.float32(DK))
        scores = jnp.where(mask == 0, jnp.float32(-1000000000.0), scores)
        attn = jax.nn.softmax(scores, axis=-1)
        out = jnp.einsum('bhqk,bhkd->bhqd', attn, v)
        out = out.transpose(0, 2, 1, 3).reshape(b, tq, c)
        return out @ Wo_w + Wo_b

    def _L1_ffn_ref(x, gate_w, w1, b1, w2, b2, sw1, sb1, sw2, sb2):
        import jax, jax.numpy as jnp
        import numpy as np
        D_MODEL = 256
        HIDDEN = 1024
        N_ROUTING = 2
        B, S, D = x.shape
        xf = x.reshape(-1, D)
        gate_scores = xf @ gate_w.T
        gate_probs = jax.nn.softmax(gate_scores, axis=-1)
        top1 = jnp.argmax(gate_probs, axis=-1)
        one_hot = jax.nn.one_hot(top1, N_ROUTING, dtype=xf.dtype)
        masked = xf[None, :, :] * one_hot.T[:, :, None]
        h = jax.nn.relu(jnp.einsum('end,edh->enh', masked, w1) + b1[:, None, :])
        expert_out = jnp.einsum('enh,ehd->end', h, w2) + b2[:, None, :]
        routing_output = expert_out.sum(axis=0)
        shared = jax.nn.relu(xf @ sw1 + sb1) @ sw2 + sb2
        return (routing_output + shared).reshape(B, S, D)
    x = x + jnp.tanh(g_xattn[0]) * _L0_xattn_ref(_layernorm(x, axis=-1), ctx_1024, ctx_1024, L0_xattn_Wq, L0_xattn_Wk, L0_xattn_Wv, L0_xattn_Wo)
    x = x + jnp.tanh(g_ffn[0]) * _L0_ffn_ref(_layernorm(x, axis=-1), L0_ffn_Wr, L0_ffn_br, L0_ffn_W1, L0_ffn_b1, L0_ffn_W2, L0_ffn_b2, L0_ffn_W3, L0_ffn_b3)
    x = x + jnp.tanh(g_xattn[1]) * _L1_xattn_ref(_layernorm(x, axis=-1), ctx_1024, ctx_1024, mask_1x1xSxS2_ik0, L1_xattn_Wq_w, L1_xattn_Wq_b, L1_xattn_Wk_w, L1_xattn_Wk_b, L1_xattn_Wv_w, L1_xattn_Wv_b, L1_xattn_Wo_w, L1_xattn_Wo_b)
    x = x + jnp.tanh(g_ffn[1]) * _L1_ffn_ref(_layernorm(x, axis=-1), L1_ffn_gate_w, L1_ffn_w1, L1_ffn_b1, L1_ffn_w2, L1_ffn_b2, L1_ffn_sw1, L1_ffn_sb1, L1_ffn_sw2, L1_ffn_sb2)
    return x

_drawn_inputs = setup_inputs


def setup_inputs(seed=0):
    import zlib

    import numpy as np

    out = dict(_drawn_inputs(seed))
    spreads = {'g_ffn': (-1.0, 0.6),
     'L0_ffn_br': (0.0, 0.8),
     'L0_ffn_b1': (0.0, 0.8),
     'L0_ffn_b2': (0.0, 0.8),
     'L0_ffn_b3': (0.0, 0.8)}
    factors = {'L0_ffn_Wr': 8.0,
     'L0_ffn_W1': 8.0,
     'L0_ffn_W2': 8.0,
     'L0_ffn_W3': 8.0,
     'L1_xattn_Wq_w': 2.952,
     'L1_xattn_Wq_b': 8.0,
     'L1_xattn_Wk_w': 2.929,
     'L1_xattn_Wk_b': 64.0,
     'L1_xattn_Wv_b': 8.0,
     'L1_xattn_Wo_b': 8.0,
     'L1_ffn_gate_w': 7.654,
     'L1_ffn_w1': 7.878,
     'L1_ffn_b1': 21.584,
     'L1_ffn_w2': 6.419,
     'L1_ffn_b2': 59.048,
     'L1_ffn_sw1': 7.902,
     'L1_ffn_sb1': 28.046,
     'L1_ffn_sw2': 6.459,
     'L1_ffn_sb2': 64.0}
    for name, (base, spread) in spreads.items():
        noise = np.random.default_rng([zlib.crc32(name.encode()), seed]).standard_normal(out[name].shape)
        drawn = base * np.exp(spread * noise) if base else spread * noise
        out[name] = jnp.asarray(drawn.astype(out[name].dtype))
    for name, factor in factors.items():
        out[name] = (out[name] * factor).astype(out[name].dtype)
    return out
```

```python
import numpy as np
from contextlib import ExitStack

import concourse.bass as bass
from concourse import mybir

F32 = mybir.dt.float32
F32R = mybir.dt.float32r
BF16 = mybir.dt.bfloat16
I32 = mybir.dt.int32
ALU = mybir.AluOpType
ACT = mybir.ActivationFunctionType
AX = mybir.AxisListType

B, S, D = 4, 512, 256
KEYS = 64
HEADS = 16
HD = D // HEADS
P = 128
T = B * S
NT = T // P
TB = S // P
C = D // P
PAIRS = HEADS // 2
HPC = HEADS // C
E0, F1, F2 = 8, 1024, 512
E1, FH = 2, 1024
M1, M2, MH = F1 // P, F2 // P, FH // P
SLOT = 256
HALVES = SLOT // P
SLOTS0 = T // SLOT + E0 - 1
SLOTS1 = T // SLOT + E1 - 1
EPS = 1e-5
MASKED = -1e9 * HD ** 0.5
SCALE = HD ** -0.5
RSQRT_SEED = 0x5F3759DF
VIS = 16
META = 32


def f32(ap):
    return ap.bitcast(F32)


def mm3(nc, out, wh, wl, xh, xl, start, stop):
    nc.tensor.matmul(out, wh, xh, start=start, stop=False)
    nc.tensor.matmul(out, wh, xl, start=False, stop=False)
    return nc.tensor.matmul(out, wl, xh, start=False, stop=stop)


def layernorm_stats(nc, dve, link, x_tiles, st, mv, var, tmp, rstd):
    n = len(x_tiles)
    for i, x in enumerate(x_tiles):
        last = nc.vector.bn_stats(st[:, i, :], x)
    link(last)
    for i in range(n):
        last = nc.vector.bn_aggr(mv[:, i, :], st[:, i, :])
    link(last)
    link(nc.vector.tensor_scalar(var, mv[:, :, 1], EPS, None, ALU.add))
    link(nc.vector.tensor_scalar(rstd.bitcast(I32), var.bitcast(I32), 1, None, ALU.logical_shift_right))
    link(nc.vector.tensor_scalar(rstd.bitcast(I32), rstd.bitcast(I32), -1.0, float(RSQRT_SEED), ALU.mult, ALU.add))
    for _ in range(3):
        link(nc.vector.tensor_tensor(tmp, rstd, rstd, ALU.mult))
        link(nc.vector.tensor_tensor(tmp, tmp, var, ALU.mult))
        link(nc.vector.tensor_scalar(tmp, tmp, -0.5, 1.5, ALU.mult, ALU.add))
        link(nc.vector.tensor_tensor(rstd, rstd, tmp, ALU.mult))


def attention_phase(nc, k, L, io):
    soft = L == 1
    E = E1 if soft else E0
    ctx = ExitStack()
    with ctx:
        def sb(name, shape, dt=F32):
            return ctx.enter_context(nc.sbuf_tensor(f"{name}_{L}", shape, dt))

        def sem(name):
            return ctx.enter_context(nc.semaphore(f"{name}_{L}"))

        w_raw = sb("w_raw", [P, 4, C, D])
        w_hi = sb("w_hi", [P, 4, C, D], F32R)
        w_lo = sb("w_lo", [P, 4, C, D], F32R)
        kT = sb("kT", [P, C, B * KEYS])
        kz_hi = sb("kz_hi", [P, B, C, HPC * KEYS], F32R)
        kz_lo = sb("kz_lo", [P, B, C, HPC * KEYS], F32R)
        vz = sb("vz", [P, B, PAIRS, 2 * HD])
        ln_st = sb("ln_st", [P, TB, 6])
        ln_mv = sb("ln_mv", [P, TB, 2])
        ln_var = sb("ln_var", [P, TB])
        ln_tmp = sb("ln_tmp", [P, TB])
        ln_rstd = sb("ln_rstd", [P, TB])
        xq = sb("xq", [P, TB, D])
        qT_hi = sb("qT_hi", [P, 2, C, S], F32R)
        qT_lo = sb("qT_lo", [P, 2, C, S], F32R)
        oT_hi = sb("oT_hi", [P, 2, C, S], F32R)
        oT_lo = sb("oT_lo", [P, 2, C, S], F32R)
        rw = sb("rw", [P, C, E])
        if soft:
            bq = sb("bq", [P, C])
            bk = sb("bk", [P, C])
            bv = sb("bv", [P, D])
            bo = sb("bo", [P, D])
            rw_hi = sb("rw_hi", [P, C, E], F32R)
            rw_lo = sb("rw_lo", [P, C, E], F32R)
            mask_i = sb("mask_i", [P, TB, KEYS], I32)
            keep = sb("keep", [P, TB, KEYS])
            fill = sb("fill", [P, TB, KEYS])
            sc = sb("sc", [P, 2, HEADS, KEYS])
            top = sb("top", [P, HEADS])
            pT = sb("pT", [P, PAIRS, S])
            den_r = sb("den_r", [P, S])
            oN = sb("oN", [P, S])
            yb = sb("yb", [P, D])
        else:
            br = sb("br", [P, E])
            prob = sb("prob", [P, 3, S])
            xrT = sb("xrT", [P, C, S])

        dve_chain = sem("dve_chain")
        x_ld = [sem(f"x_ld{b}") for b in range(B)]
        w_ld, c_ld = sem("w_ld"), sem("c_ld")
        wh_ok, wl_ok, kp_done, kT_ok, kzh_ok, kzl_ok = (sem(n) for n in ("wh_ok", "wl_ok", "kp_done", "kT_ok", "kzh_ok", "kzl_ok"))
        vp_done, vz_ok = sem("vp_done"), sem("vz_ok")
        xn_ok, tr_done, th_ok, tl_ok = (sem(n) for n in ("xn_ok", "tr_done", "th_ok", "tl_ok"))
        q_done, qh_ok, ql_ok = sem("q_done"), sem("qh_ok"), sem("ql_ok")
        s_done, p_ok, pv_done, oh_ok, ol_ok = (sem(n) for n in ("s_done", "p_ok", "pv_done", "oh_ok", "ol_ok"))
        y_done, y_used, lg_done, lg_ok = (sem(n) for n in ("y_done", "y_used", "lg_done", "lg_ok"))
        xr_ok, vz0 = sem("xr_ok"), sem("vz0")
        if soft:
            s_used, sm_ok, pt_done, pt_ok, rw_ok, fill_ok, den_ok = (sem(n) for n in ("s_used", "sm_ok", "pt_done", "pt_ok", "rw_ok", "fill_ok", "den_ok"))
        if not soft:
            i_ok, mk_ok, tg_ok, g_ld, ctx_ld, ctxh_ok, ctxl_ok, z_ok, z_st = (sem(n) for n in ("i_ok", "mk_ok", "tg_ok", "g_ld", "ctx_ld", "ctxh_ok", "ctxl_ok", "z_ok", "z_st"))
        WQ, WK, WV, WO = range(4)
        ps = k["ps"]
        STEPS = B + 2
        CLD = 16 * (6 if soft else 2)

        block = ctx.enter_context(nc.Block())

        @block.sync
        def _(sp):
            if not soft:
                for b in range(B):
                    sp.dma_start(k["x"][:, b * TB:(b + 1) * TB, :], io["x"][b]).then_inc(x_ld[b], 16)
                    if b == 0:
                        sp.dma_start(k["ctx_raw"][:], io["ctx"]).then_inc(ctx_ld, 16)
                        sp.dma_start(w_raw[:], io["wa"][L]).then_inc(w_ld, 16)
                sp.dma_start(k["g_raw"][:], io["g"]).then_inc(g_ld, 16)
                sp.dma_start(br[:], io["br"]).then_inc(c_ld, 16)
                sp.dma_start(rw[:], io["rw"][L]).then_inc(c_ld, 16)
                sp.wait_ge(z_ok, 1)
                nz = 0
                for scratch in ("xs0", "ys0", "xs1", "ys1"):
                    rows = k[scratch].shape[0]
                    for a in range(0, rows, 1024):
                        n = min(1024, rows - a)
                        sp.dma_start(k[scratch][a:a + n, :].rearrange("(p r) d -> p (r d)", p=P),
                                     k["zeros"][:, 0:n // P * D]).then_inc(z_st, 16)
                        nz += 16
                sp.wait_ge(z_st, nz)
            else:
                sp.dma_start(w_raw[:], io["wa"][L]).then_inc(w_ld, 16)
                for dst, src in ((bq, "bq"), (bk, "bk"), (bv, "bv"), (bo, "bo"), (mask_i, "mask")):
                    sp.dma_start(dst[:], io[src]).then_inc(c_ld, 16)
                sp.dma_start(rw[:], io["rw"][L]).then_inc(c_ld, 16)

        @block.gpsimd
        def _(pool):
            if not soft:
                nc.gpsimd.memset(k["ident"][:], 0.0).then_inc(i_ok, 1)
                nc.gpsimd.memset(k["head_rows"][:], 1.0).then_inc(i_ok, 1)
                nc.gpsimd.memset(k["below"][:], 1.0).then_inc(i_ok, 1)
                pool.wait_ge(i_ok, 3)
                nc.gpsimd.affine_select(out=k["ident"][:], in_=k["ident"][:], compare_op=ALU.not_equal, fill=1.0,
                                        base=0, pattern=[[-1, P]], channel_multiplier=1).then_inc(i_ok, 1)
                nc.gpsimd.affine_select(out=k["head_rows"][:], in_=k["head_rows"][:], compare_op=ALU.is_ge, fill=0.0,
                                        base=0, pattern=[[-HD, HPC]], channel_multiplier=1).then_inc(i_ok, 1)
                pool.wait_ge(i_ok, 5)
                nc.gpsimd.affine_select(out=k["head_rows"][:], in_=k["head_rows"][:], compare_op=ALU.is_ge, fill=0.0,
                                        base=HD - 1, pattern=[[HD, HPC]], channel_multiplier=-1).then_inc(mk_ok, 1)
                nc.gpsimd.affine_select(out=k["below"][:], in_=k["below"][:], compare_op=ALU.is_gt, fill=0.0,
                                        base=0, pattern=[[1, P]], channel_multiplier=-1).then_inc(mk_ok, 1)
                nc.gpsimd.memset(k["zeros"][:], 0.0).then_inc(z_ok, 1)
                nc.gpsimd.memset(k["ones_b"][:], 1.0).then_inc(mk_ok, 1)
                nc.gpsimd.memset(k["den_w"][:], 0.0).then_inc(mk_ok, 1)
                pool.wait_ge(mk_ok, 4)
                nc.gpsimd.memset(k["den_w"][0:KEYS, 0:HD], 1.0).then_inc(mk_ok, 1)
                pool.wait_ge(mk_ok, 5)
                nc.gpsimd.memset(k["den_w"][KEYS:P, HD:2 * HD], 1.0).then_inc(mk_ok, 1)
                pool.wait_ge(mk_ok, 6)
            nc.gpsimd.memset(vz[:], 0.0).then_inc(vz0, 1)
            if soft:
                for n in range(NT):
                    if n == 0:
                        pool.wait_ge(fill_ok, 1)
                    pool.wait_ge(s_used, 2 * n + 1)
                    nc.gpsimd.tensor_tensor(sc[:, n % 2], sc[:, n % 2],
                                            fill[:, n % TB, None, :].to_broadcast([P, HEADS, KEYS]), ALU.add).then_inc(sm_ok, 1)

        @block.scalar
        def _(act):
            def to_hi(dst, src, done, waits):
                for s_, v_ in waits:
                    act.wait_ge(s_, v_)
                nc.scalar.activation(dst, src, ACT.Copy).then_inc(done, 1)

            if not soft:
                to_hi(k["ctx_hi"][:], k["ctx_raw"][:, :, :, None, :].to_broadcast([P, C, B, 2, KEYS]), ctxh_ok, [(ctx_ld, 16)])
            to_hi(w_hi[:], w_raw[:], wh_ok, [(w_ld, 16)])
            if not soft:
                act.wait_ge(g_ld, 16)
                nc.scalar.activation(k["tg"][:], k["g_raw"][:], ACT.Tanh).then_inc(tg_ok, 1)

            act.wait_ge(kp_done, 1)
            if soft:
                act.wait_ge(c_ld, CLD)
                for m in range(C):
                    last = nc.scalar.activation(kT[:, m, :], ps[:, 4 + m, 0:B * KEYS], ACT.Identity, bias=bk[:, m:m + 1])
            else:
                last = nc.scalar.activation(kT[:], ps[:, 4:6, 0:B * KEYS], ACT.Copy)
            last.then_inc(kT_ok, 1)
            act.wait_ge(kT_ok, 1)
            if not soft:
                act.wait_ge(mk_ok, 6)
            for c in range(C):
                for h in range(HPC):
                    nc.scalar.activation(kz_hi[:, :, c, h * KEYS:(h + 1) * KEYS],
                                         kT[:, c, :].rearrange("p (b n) -> p b n", b=B), ACT.Copy,
                                         scale=k["head_rows"][:, h:h + 1]).then_inc(kzh_ok, 1)

            trn = [0]

            def transposed_hi(dst):
                trn[0] += 1
                act.wait_ge(tr_done, trn[0])
                nc.scalar.activation(dst, ps[:, 0:2, :], ACT.Copy).then_inc(th_ok, 1)

            def attend(b):
                for j in range(PAIRS):
                    n = b * PAIRS + j
                    act.wait_ge(s_done, n + 1)
                    if n >= 3:
                        act.wait_ge(pv_done, n - 2)
                    nc.scalar.activation(prob[:, n % 3, :], ps[:, 4 + n % 2, :], ACT.Sigmoid, scale=SCALE).then_inc(p_ok, 1)

            def attend_soft(b):
                for i in range(TB):
                    n = b * TB + i
                    act.wait_ge(s_used, 2 * n + 2)
                    nc.scalar.activation(sc[:, n % 2], sc[:, n % 2], ACT.Exp, scale=SCALE).then_inc(p_ok, 1)
                    act.wait_ge(pt_done, n + 1)
                    if i == 0 and b:
                        act.wait_ge(pv_done, b)
                    nc.scalar.activation(pT[:, 0:4, i * P:(i + 1) * P], ps[:, 4, :].rearrange("p (j q) -> p j q", j=4), ACT.Copy).then_inc(pt_ok, 1)

            for s in range(STEPS):
                if s < B:
                    transposed_hi(k["xT_hi"][:, :, s * S:(s + 1) * S])
                    act.wait_ge(q_done, s + 1)
                    if s >= 2:
                        act.wait_ge(s_done, (TB if soft else PAIRS) * (s - 1))
                    if soft:
                        for m in range(C):
                            last = nc.scalar.activation(qT_hi[:, s % 2, m], ps[:, 2 + m, :], ACT.Identity, bias=bq[:, m:m + 1])
                    else:
                        last = nc.scalar.activation(qT_hi[:, s % 2], ps[:, 2:4, :], ACT.Copy)
                    last.then_inc(qh_ok, 1)
                if 1 <= s < B + 1:
                    if soft:
                        attend_soft(s - 1)
                    else:
                        attend(s - 1)
                if s >= 2:
                    if soft:
                        b = s - 2
                        transposed_hi(k["xT_hi"][:, :, b * S:(b + 1) * S])
                    else:
                        trn[0] += 1
                        act.wait_ge(tr_done, trn[0])
                        if s > 2:
                            act.wait_ge(lg_done, s - 2)
                        nc.scalar.activation(xrT[:], ps[:, 0:2, :], ACT.Copy).then_inc(xr_ok, 1)

        @block.vector
        def _(dve):
            chain = [0]

            def link(ins):
                chain[0] += 1
                ins.then_inc(dve_chain, 1)
                dve.wait_ge(dve_chain, chain[0])

            def normalise(tiles, dst, done):
                layernorm_stats(nc, dve, link, [k["x"][:, t, :] for t in tiles], ln_st, ln_mv, ln_var[:], ln_tmp[:], ln_rstd[:])
                for i, t in enumerate(tiles):
                    last = nc.vector.tensor_scalar(dst(i, t), k["x"][:, t, :], ln_mv[:, i, 0:1], ln_rstd[:, i:i + 1],
                                                   ALU.subtract, ALU.mult)
                last.then_inc(done, 1)
                dve.wait_ge(done, normalise.n + 1)
                normalise.n += 1
            normalise.n = 0

            thn = [0]

            def front(b):
                if not soft:
                    dve.wait_ge(x_ld[b], 16)
                if b:
                    dve.wait_ge(q_done, b)
                normalise(range(b * TB, (b + 1) * TB), lambda i, t: xq[:, i, :], xn_ok)
                thn[0] += 1
                transposed_lo(b)
                dve.wait_ge(qh_ok, b + 1)
                if soft:
                    for m in range(C):
                        last = nc.vector.scalar_tensor_tensor(out=qT_lo[:, b % 2, m], in0=ps[:, 2 + m, :], scalar=bq[:, m:m + 1],
                                                              in1=f32(qT_hi[:, b % 2, m]), op0=ALU.add, op1=ALU.subtract)
                else:
                    last = nc.vector.tensor_tensor(qT_lo[:, b % 2], ps[:, 2:4, :], f32(qT_hi[:, b % 2]), ALU.subtract)
                last.then_inc(ql_ok, 1)

            def transposed_lo(b):
                dve.wait_ge(th_ok, thn[0])
                nc.vector.tensor_tensor(k["xT_lo"][:, :, b * S:(b + 1) * S], ps[:, 0:2, :],
                                        f32(k["xT_hi"][:, :, b * S:(b + 1) * S]), ALU.subtract).then_inc(tl_ok, 1)

            def attend(b):
                for c in range(C):
                    dve.wait_ge(pv_done, b * PAIRS + (c + 1) * PAIRS // C)
                    if b >= 2 and c == 0:
                        dve.wait_ge(y_done, TB * (b - 1))
                    link(nc.vector.tensor_copy(oT_hi[:, b % 2, c], ps[:, 6 + c, :]))
                    nc.vector.tensor_tensor(oT_lo[:, b % 2, c], ps[:, 6 + c, :], f32(oT_hi[:, b % 2, c]), ALU.subtract).then_inc(ol_ok, 1)

            def attend_soft(b):
                def second_half(n, i):
                    dve.wait_ge(pt_done, n + 1)
                    nc.vector.tensor_copy(pT[:, 4:8, i * P:(i + 1) * P], ps[:, 5, :].rearrange("p (j q) -> p j q", j=4)).then_inc(pt_ok, 1)

                for i in range(TB):
                    n = b * TB + i
                    dve.wait_ge(s_done, n + 1)
                    if n >= 2:
                        dve.wait_ge(pt_done, n - 1)
                    nc.vector.tensor_tensor(sc[:, n % 2], ps[:, 6:8, :].rearrange("p c (h n) -> p (c h) n", h=HPC),
                                            keep[:, i, None, :].to_broadcast([P, HEADS, KEYS]), ALU.mult).then_inc(s_used, 1)
                    if i:
                        second_half(n - 1, i - 1)
                    dve.wait_ge(sm_ok, n + 1)
                    link(nc.vector.tensor_reduce(top[:], sc[:, n % 2], AX.X, ALU.max))
                    nc.vector.tensor_tensor(sc[:, n % 2], sc[:, n % 2], top[:, :, None].to_broadcast([P, HEADS, KEYS]),
                                            ALU.subtract).then_inc(s_used, 1)
                second_half(b * TB + TB - 1, TB - 1)
                dve.wait_ge(pv_done, b + 1)
                for c in range(C):
                    link(nc.vector.reciprocal(den_r[:], ps[:, 4 + c, :]))
                    link(nc.vector.tensor_tensor(oN[:], ps[:, 6 + c, :], den_r[:], ALU.mult))
                    if b >= 2 and c == 0:
                        dve.wait_ge(y_done, TB * (b - 1))
                    link(nc.vector.tensor_copy(oT_hi[:, b % 2, c], oN[:]))
                    last = nc.vector.tensor_tensor(oT_lo[:, b % 2, c], oN[:], f32(oT_hi[:, b % 2, c]), ALU.subtract)
                last.then_inc(ol_ok, 1)

            def back(b):
                for i in range(TB):
                    n = b * TB + i
                    dve.wait_ge(y_done, n + 1)
                    if n == 0 and not soft:
                        dve.wait_ge(tg_ok, 1)
                    if soft:
                        nc.vector.tensor_tensor(yb[:], ps[:, 2 + n % 2, 0:D], bo[:], ALU.add).then_inc(y_used, 1)
                        dve.wait_ge(y_used, n + 1)
                        link(nc.vector.scalar_tensor_tensor(out=k["x"][:, n, :], in0=yb[:], scalar=k["tg"][:, L:L + 1],
                                                            in1=k["x"][:, n, :], op0=ALU.mult, op1=ALU.add))
                    else:
                        nc.vector.scalar_tensor_tensor(out=k["x"][:, n, :], in0=ps[:, 2 + n % 2, 0:D], scalar=k["tg"][:, L:L + 1],
                                                       in1=k["x"][:, n, :], op0=ALU.mult, op1=ALU.add).then_inc(y_used, 1)
                dve.wait_ge(y_used, (b + 1) * TB)
                normalise(range(b * TB, (b + 1) * TB), lambda i, t: k["xn"][:, t, :], xn_ok)
                if soft:
                    thn[0] += 1
                    transposed_lo(b)
                dve.wait_ge(lg_done, b + 1)
                lg = ps[:, 2, 0:TB * E].rearrange("p (i e) -> p i e", e=E)
                if soft:
                    last = nc.vector.tensor_copy(k["lg1"][:, b * TB:(b + 1) * TB, :], lg)
                else:
                    last = nc.vector.tensor_tensor(k["lg0"][:, b * TB:(b + 1) * TB, :], lg, br[:, None, :].to_broadcast([P, TB, E]), ALU.add)
                last.then_inc(lg_ok, 1)

            if not soft:
                dve.wait_ge(ctxh_ok, 1)
                nc.vector.tensor_tensor(k["ctx_lo"][:].rearrange("p c b t n -> p (c b) t n"),
                                        k["ctx_raw"][:].rearrange("p c b n -> p (c b) n")[:, :, None, :].to_broadcast([P, C * B, 2, KEYS]),
                                        f32(k["ctx_hi"][:].rearrange("p c b t n -> p (c b) t n")), ALU.subtract).then_inc(ctxl_ok, 1)
            dve.wait_ge(wh_ok, 1)
            nc.vector.tensor_tensor(w_lo[:], w_raw[:], f32(w_hi[:]), ALU.subtract).then_inc(wl_ok, 1)
            dve.wait_ge(c_ld, CLD)
            if soft:
                link(nc.vector.tensor_copy(rw_hi[:], rw[:]))
                nc.vector.tensor_tensor(rw_lo[:], rw[:], f32(rw_hi[:]), ALU.subtract).then_inc(rw_ok, 1)
                link(nc.vector.tensor_scalar(keep[:], mask_i[:], 0.0, None, ALU.not_equal))
                nc.vector.tensor_scalar(fill[:], keep[:], 1.0, -MASKED, ALU.subtract, ALU.mult).then_inc(fill_ok, 1)
            for c in range(C):
                for h in range(HPC):
                    dve.wait_ge(kzh_ok, c * HPC + h + 1)
                    nc.vector.scalar_tensor_tensor(out=kz_lo[:, :, c, h * KEYS:(h + 1) * KEYS],
                                                   in0=kT[:, c, :].rearrange("p (b n) -> p b n", b=B), scalar=k["head_rows"][:, h:h + 1],
                                                   in1=f32(kz_hi[:, :, c, h * KEYS:(h + 1) * KEYS]),
                                                   op0=ALU.mult, op1=ALU.subtract).then_inc(kzl_ok, 1)
            dve.wait_ge(vz0, 1)
            for b in range(B):
                dve.wait_ge(vp_done, b + 1)
                src = ps[:, 6 + b % 2, 0:D].rearrange("p (j a d) -> p j a d", a=2, d=HD)
                for a in range(2):
                    r = slice(a * KEYS, (a + 1) * KEYS)
                    if soft:
                        last = nc.vector.tensor_tensor(vz[r, b, :, a * HD:(a + 1) * HD], src[r, :, a, :],
                                                       bv[r, :].rearrange("p (j a d) -> p j a d", a=2, d=HD)[:, :, a, :], ALU.add)
                    else:
                        last = nc.vector.tensor_copy(vz[r, b, :, a * HD:(a + 1) * HD], src[r, :, a, :])
                last.then_inc(vz_ok, 1)

            for s in range(STEPS):
                if s < B:
                    front(s)
                if 1 <= s < B + 1:
                    if soft:
                        attend_soft(s - 1)
                    else:
                        attend(s - 1)
                if s >= 2:
                    back(s - 2)

        @block.tensor
        def _(pe):
            tn = [0, 0]

            def eight_transposes(src, ready):
                pe.wait_ge(xn_ok, ready)
                if tn[0]:
                    pe.wait_ge(tl_ok, tn[0] - tn[1])
                if tn[1]:
                    pe.wait_ge(xr_ok, tn[1])
                for c in range(C):
                    for i in range(TB):
                        last = nc.tensor.transpose(ps[:, c, i * P:(i + 1) * P], src(i, c), k["ident"][:])
                last.then_inc(tr_done, 1)
                tn[0] += 1

            def front(b):
                eight_transposes(lambda i, c: xq[:, i, c * P:(c + 1) * P], tn[0] + 1)
                pe.wait_ge(tl_ok, tn[0] - tn[1])
                if b:
                    pe.wait_ge(ql_ok, b)
                if b >= 3:
                    pe.wait_ge(lg_ok, b - 2)
                for m in range(C):
                    for c in range(C):
                        w = slice(m * P, (m + 1) * P)
                        last = mm3(nc, ps[:, 2 + m, :], w_hi[:, WQ, c, w], w_lo[:, WQ, c, w],
                                   k["xT_hi"][:, c, b * S:(b + 1) * S], k["xT_lo"][:, c, b * S:(b + 1) * S], c == 0, c == C - 1)
                last.then_inc(q_done, 1)

            def attend(b):
                pe.wait_ge(ql_ok, b + 1)
                for j in range(PAIRS + 1):
                    n = b * PAIRS + j
                    if j < PAIRS:
                        if n >= 2:
                            pe.wait_ge(p_ok, n - 1)
                        c, o = j // 4, (j % 4) * P
                        last = mm3(nc, ps[:, 4 + n % 2, :], kz_hi[:, b, c, o:o + P], kz_lo[:, b, c, o:o + P],
                                   qT_hi[:, b % 2, c], qT_lo[:, b % 2, c], True, True)
                        last.then_inc(s_done, 1)
                    if j:
                        jj = j - 1
                        pe.wait_ge(p_ok, n)
                        if jj % 4 == 0 and b:
                            pe.wait_ge(ol_ok, C * (b - 1) + jj // 4 + 1)
                        r = 2 * HD * (jj % 4)
                        nc.tensor.matmul(ps[r:r + 2 * HD, 6 + jj // 4, :], vz[:, b, jj, :], prob[:, (n - 1) % 3, :],
                                         start=True, stop=True).then_inc(pv_done, 1)

            def attend_soft(b):
                pe.wait_ge(ql_ok, b + 1)
                if b:
                    pe.wait_ge(ol_ok, b)

                def scores(i):
                    n = b * TB + i
                    if i:
                        pe.wait_ge(s_used, 2 * n - 1)
                    for c in range(C):
                        last = mm3(nc, ps[:, 6 + c, :], qT_hi[:, b % 2, c, i * P:(i + 1) * P], qT_lo[:, b % 2, c, i * P:(i + 1) * P],
                                   kz_hi[:, b, c, :], kz_lo[:, b, c, :], True, True)
                    last.then_inc(s_done, 1)

                scores(0)
                for i in range(TB):
                    n = b * TB + i
                    if i + 1 < TB:
                        scores(i + 1)
                    pe.wait_ge(p_ok, n + 1)
                    if i:
                        pe.wait_ge(pt_ok, 2 * n)
                    for j in range(PAIRS):
                        last = nc.tensor.transpose(ps[:, 4 + j // 4, (j % 4) * P:(j % 4 + 1) * P],
                                                   sc[:, n % 2, 2 * j:2 * j + 2, :].rearrange("p h n -> p (h n)"), k["ident"][:])
                    last.then_inc(pt_done, 1)
                pe.wait_ge(pt_ok, 2 * TB * (b + 1))
                for j in range(PAIRS):
                    r, c = 2 * HD * (j % 4), j // 4
                    nc.tensor.matmul(ps[r:r + 2 * HD, 6 + c, :], vz[:, b, j, :], pT[:, j, :], start=True, stop=True)
                for j in range(PAIRS):
                    r, c = 2 * HD * (j % 4), j // 4
                    last = nc.tensor.matmul(ps[r:r + 2 * HD, 4 + c, :], k["den_w"][:], pT[:, j, :], start=True, stop=True)
                last.then_inc(pv_done, 1)

            def back(b):
                pe.wait_ge(ol_ok, (1 if soft else C) * (b + 1))
                pe.wait_ge(ql_ok, min(b + 3, B))
                for i in range(TB):
                    n = b * TB + i
                    if n >= 2:
                        pe.wait_ge(y_used, n - 1)
                    if i == 0 and b:
                        pe.wait_ge(lg_ok, b)
                    for c in range(C):
                        t = slice(i * P, (i + 1) * P)
                        last = mm3(nc, ps[:, 2 + n % 2, 0:D], oT_hi[:, b % 2, c, t], oT_lo[:, b % 2, c, t],
                                   w_hi[:, WO, c, :], w_lo[:, WO, c, :], c == 0, c == C - 1)
                    last.then_inc(y_done, 1)
                eight_transposes(lambda i, c: k["xn"][:, b * TB + i, c * P:(c + 1) * P], tn[0] + 1)
                if not soft:
                    tn[1] += 1
                    pe.wait_ge(xr_ok, tn[1])
                    for i in range(TB):
                        for c in range(C):
                            last = nc.tensor.matmul(ps[:, 2, i * E:(i + 1) * E], xrT[:, c, i * P:(i + 1) * P], rw[:, c, :],
                                                    start=c == 0, stop=c == C - 1)
                else:
                    pe.wait_ge(tl_ok, tn[0])
                    for i in range(TB):
                        t = slice(b * S + i * P, b * S + (i + 1) * P)
                        for c in range(C):
                            last = mm3(nc, ps[:, 2, i * E:(i + 1) * E], k["xT_hi"][:, c, t], k["xT_lo"][:, c, t],
                                       rw_hi[:, c, :], rw_lo[:, c, :], c == 0, c == C - 1)
                last.then_inc(lg_done, 1)

            pe.wait_ge(wl_ok, 1)
            if not soft:
                pe.wait_ge(ctxl_ok, 1)
            for m in range(C):
                for c in range(C):
                    w = slice(m * P, (m + 1) * P)
                    last = mm3(nc, ps[:, 4 + m, 0:B * KEYS], w_hi[:, WK, c, w], w_lo[:, WK, c, w],
                               k["ctx_hi"][:, c, :, 0, :], k["ctx_lo"][:, c, :, 0, :], c == 0, c == C - 1)
            last.then_inc(kp_done, 1)
            for b in range(B):
                if b >= 2:
                    pe.wait_ge(vz_ok, b - 1)
                for c in range(C):
                    last = mm3(nc, ps[:, 6 + b % 2, 0:D], k["ctx_hi"][:, c, b].rearrange("p t n -> p (t n)"),
                               k["ctx_lo"][:, c, b].rearrange("p t n -> p (t n)"), w_hi[:, WV, c, :], w_lo[:, WV, c, :], c == 0, c == C - 1)
                last.then_inc(vp_done, 1)
            if soft:
                pe.wait_ge(rw_ok, 1)
            else:
                pe.wait_ge(c_ld, CLD)
                pe.wait_ge(i_ok, 5)
                pe.wait_ge(mk_ok, 6)
            for s in range(STEPS):
                if s < B:
                    front(s)
                if s == 1:
                    pe.wait_ge(kT_ok, 1)
                    pe.wait_ge(kzl_ok, HEADS)
                    pe.wait_ge(vz_ok, B)
                if 1 <= s < B + 1:
                    if soft:
                        attend_soft(s - 1)
                    else:
                        attend(s - 1)
                if s >= 2:
                    back(s - 2)


def routing_phase(nc, k, L):
    E = E1 if L else E0
    lg, pos, meta, xs = (k[f"{n}{L}"] for n in ("lg", "pos", "meta", "xs"))
    ctx = ExitStack()
    with ctx:
        def sb(name, shape, dt=F32):
            return ctx.enter_context(nc.sbuf_tensor(f"r_{name}_{L}", shape, dt))

        def sem(name):
            return ctx.enter_context(nc.semaphore(f"r_{name}_{L}"))

        top = sb("top", [P, NT])
        eq = sb("eq", [P, NT, E])
        rank = sb("rank", [P, E])
        oh = sb("oh", [P, NT, E])
        oh_b = sb("oh_b", [P, NT, E], BF16)
        tot = sb("tot", [P, E, NT])
        inside = sb("inside", [P, E, NT])
        upto = sb("upto", [P, E, NT])
        step = sb("step", [P, T // SLOT])
        over = sb("over", [P, E, T // SLOT])
        slots = sb("slots", [P, E])
        some = sb("some", [P, E])
        ends = sb("ends", [P, E + 1])
        seen = sb("seen", [P, E + 1])
        ones = sb("ones", [P, E])
        place = sb("place", [P, NT, E])
        posf = sb("posf", [P, NT])
        chain_s, consts, oh_ok, pre_ok, pos_ok, scat, exp_in, exp_ok = (
            sem(n) for n in ("chain", "consts", "oh_ok", "pre_ok", "pos_ok", "scat", "exp_in", "exp_ok"))
        ps = k["ps"]
        block = ctx.enter_context(nc.Block())

        @block.gpsimd
        def _(pool):
            for e in range(E):
                nc.gpsimd.memset(rank[:, e:e + 1], float(E - e)).then_inc(consts, 1)
            for j in range(T // SLOT):
                nc.gpsimd.memset(step[:, j:j + 1], float(j * SLOT)).then_inc(consts, 1)
            nc.gpsimd.memset(ones[:], 1.0).then_inc(consts, 1)
            nc.gpsimd.memset(ends[:, 0:1], 0.0).then_inc(consts, 1)
            nc.gpsimd.memset(seen[:, 0:1], 0.0).then_inc(consts, 1)
            nc.gpsimd.memset(meta[:], 0).then_inc(consts, 1)
            nc.gpsimd.memset(inside[:], 1.0).then_inc(consts, 1)
            pool.wait_ge(consts, E + T // SLOT + 5)
            nc.gpsimd.memset(inside[:, :, 0:1], 0.0).then_inc(consts, 1)
            pool.wait_ge(pos_ok, 1)
            for t in range(NT):
                pool.indirect_dma_start(out=xs, out_offset=bass.IndirectOffsetOnAxis(ap=pos[:, t:t + 1], axis=0),
                                        in_=k["xn"][:, t, :], in_offset=None).then_inc(scat, 16)
            pool.wait_ge(scat, 16 * NT)

        @block.scalar
        def _(act):
            if L:
                act.wait_ge(exp_in, 1)
                nc.scalar.activation(eq[:], eq[:], ACT.Exp).then_inc(exp_ok, 1)

        @block.vector
        def _(dve):
            chain = [0]

            def link(ins):
                chain[0] += 1
                ins.then_inc(chain_s, 1)
                dve.wait_ge(chain_s, chain[0])

            def first_best(src):
                link(nc.vector.tensor_reduce(top[:], src, AX.X, ALU.max))
                link(nc.vector.tensor_tensor(eq[:], src, top[:, :, None].to_broadcast([P, NT, E]), ALU.is_ge))
                link(nc.vector.tensor_tensor(eq[:], eq[:], rank[:, None, :].to_broadcast([P, NT, E]), ALU.mult))
                link(nc.vector.tensor_reduce(top[:], eq[:], AX.X, ALU.max))
                link(nc.vector.tensor_tensor(oh[:], eq[:], top[:, :, None].to_broadcast([P, NT, E]), ALU.is_ge))

            dve.wait_ge(consts, E + T // SLOT + 6)
            if L:
                link(nc.vector.tensor_reduce(top[:], lg[:], AX.X, ALU.max))
                nc.vector.tensor_tensor(eq[:], lg[:], top[:, :, None].to_broadcast([P, NT, E]), ALU.subtract).then_inc(exp_in, 1)
                dve.wait_ge(exp_ok, 1)
                link(nc.vector.tensor_copy(lg[:], eq[:]))
            first_best(lg[:])
            nc.vector.tensor_copy(oh_b[:], oh[:]).then_inc(oh_ok, 1)
            dve.wait_ge(pre_ok, 1)
            link(nc.vector.tensor_copy(tot[:], ps[:, 1, 0:NT * E].rearrange("p (t e) -> p e t", e=E)))
            link(nc.vector.tensor_tensor_scan(upto[:].rearrange("p e t -> p (e t)"), inside[:].rearrange("p e t -> p (e t)"),
                                              tot[:].rearrange("p e t -> p (e t)"), 0.0, ALU.mult, ALU.add))
            link(nc.vector.tensor_tensor(over[:], upto[:, :, NT - 1:NT].to_broadcast([P, E, T // SLOT]),
                                         step[:, None, :].to_broadcast([P, E, T // SLOT]), ALU.is_gt))
            link(nc.vector.tensor_reduce(slots[:], over[:], AX.X, ALU.add))
            link(nc.vector.tensor_scalar(some[:], slots[:], 0.0, None, ALU.is_gt))
            link(nc.vector.tensor_tensor_scan(ends[:, 1:E + 1], ones[:], slots[:], 0.0, ALU.mult, ALU.add))
            link(nc.vector.tensor_tensor_scan(seen[:, 1:E + 1], ones[:], some[:], 0.0, ALU.mult, ALU.add))
            link(nc.vector.tensor_copy(meta[0:1, 0:E + 1], ends[0:1, :]))
            link(nc.vector.tensor_copy(meta[0:1, VIS:VIS + E + 1], seen[0:1, :]))
            link(nc.vector.tensor_tensor(tot[:], upto[:], tot[:], ALU.subtract))
            link(nc.vector.tensor_scalar(slots[:], ends[:, 0:E], float(SLOT), None, ALU.mult))
            link(nc.vector.tensor_tensor(tot[:], tot[:], slots[:, :, None].to_broadcast([P, E, NT]), ALU.add))
            link(nc.vector.tensor_tensor(place[:], ps[:, 0, 0:NT * E].rearrange("p (t e) -> p t e", e=E),
                                         tot[:].rearrange("p e t -> p t e"), ALU.add))
            link(nc.vector.tensor_tensor(place[:], place[:], oh[:], ALU.mult))
            link(nc.vector.tensor_reduce(posf[:], place[:], AX.X, ALU.add))
            nc.vector.tensor_copy(pos[:], posf[:]).then_inc(pos_ok, 1)

        @block.tensor
        def _(pe):
            pe.wait_ge(oh_ok, 1)
            rows = oh_b[:].rearrange("p t e -> p (t e)")
            nc.tensor.matmul(ps[:, 0, 0:NT * E], k["below"][:], rows, start=True, stop=True)
            nc.tensor.matmul(ps[:, 1, 0:NT * E], k["ones_b"][:], rows, start=True, stop=True).then_inc(pre_ok, 1)


def slots_of(eng, meta, e, most):
    n0 = eng.value_load(meta[0:1, bass.ds(e, 1)], min_val=0, max_val=most - 1)
    n1 = eng.value_load(meta[0:1, bass.ds(e + 1, 1)], min_val=0, max_val=most)
    v = eng.value_load(meta[0:1, bass.ds(e + VIS, 1)], min_val=0, max_val=E0)
    return n0, n1, v


def experts_phase(nc, k, io):
    BL = M1 + M2
    ctx = ExitStack()
    with ctx:
        def sb(name, shape, dt=F32):
            return ctx.enter_context(nc.sbuf_tensor(f"e_{name}", shape, dt))

        def sem(name):
            return ctx.enter_context(nc.semaphore(f"e_{name}"))

        w1_raw, w2_raw, w3_raw = sb("w1_raw", [P, C, F1]), sb("w2_raw", [P, M1, F2]), sb("w3_raw", [P, M2, D])
        w1_hi, w2_hi, w3_hi = sb("w1_hi", [P, C, F1], F32R), sb("w2_hi", [P, M1, F2], F32R), sb("w3_hi", [P, M2, D], F32R)
        w1_lo, w2_lo, w3_lo = sb("w1_lo", [P, C, F1], F32R), sb("w2_lo", [P, M1, F2], F32R), sb("w3_lo", [P, M2, D], F32R)
        b1, b2, b3 = sb("b1", [P, E0 * M1]), sb("b2", [P, E0 * M2]), sb("b3", [P, E0 * D])
        xg = sb("xg", [P, HALVES, D])
        gT_hi, gT_lo = sb("gT_hi", [P, C, SLOT], F32R), sb("gT_lo", [P, C, SLOT], F32R)
        h32 = sb("h32", [P, 2, SLOT])
        h_hi, h_lo = sb("h_hi", [P, BL, SLOT], F32R), sb("h_lo", [P, BL, SLOT], F32R)
        yo = sb("yo", [P, HALVES, D])
        tick, tick_ok = sb("tick", [P, 3]), sem("tick_ok")
        b_ld, w1_ld, w2_ld, w3_ld, xg_ld, y_st = (sem(n) for n in ("b_ld", "w1_ld", "w2_ld", "w3_ld", "xg_ld", "y_st"))
        w1h_ok, w1l_ok, w2h_ok, w2l_ok, w3h_ok, w3l_ok = (sem(n) for n in ("w1h_ok", "w1l_ok", "w2h_ok", "w2l_ok", "w3h_ok", "w3l_ok"))
        gt_done, gh_ok, gl_ok, hb_done = (sem(n) for n in ("gt_done", "gh_ok", "gl_ok", "hb_done"))
        gelu_ok, hh_ok, hl_ok, y_done, y_used = (sem(n) for n in ("gelu_ok", "hh_ok", "hl_ok", "y_done", "y_used"))
        ps, meta, xs, ys = k["ps"], k["meta0"], k["xs0"], k["ys0"]
        xs_v = xs.rearrange("(s t p) d -> s p t d", p=P, t=HALVES)
        block = ctx.enter_context(nc.Block())

        @block.sync
        def _(sp):
            for dst, src in ((b1, "b1"), (b2, "b2"), (b3, "b3")):
                sp.dma_start(dst[:], io[src]).then_inc(b_ld, 16)
            with sp.Fori(0, E0) as e:
                n0, n1, v = slots_of(sp, meta, e, SLOTS0)
                with sp.If(n0 < n1):
                    sp.wait_ge(w1l_ok, v + 1)
                    sp.dma_start(w1_raw[:], io["W1"][bass.ds(e * P, P)]).then_inc(w1_ld, 16)
                    sp.wait_ge(w2l_ok, v * M1 + 1)
                    sp.dma_start(w2_raw[:], io["W2"][bass.ds(e * P, P)]).then_inc(w2_ld, 16)
                    sp.wait_ge(w3l_ok, v + 1)
                    sp.dma_start(w3_raw[:], io["W3"][bass.ds(e * P, P)]).then_inc(w3_ld, 16)
                sp.end_ifs()

        @block.gpsimd
        def _(pool):
            def slot(s, v=None, n0=None):
                pool.wait_ge(gt_done, s + 1)
                pool.dma_start(xg[:], xs[bass.ds((s + 1) * SLOT, SLOT), :].rearrange("(t p) d -> p t d", p=P)).then_inc(xg_ld, 16)
                if v is not None:
                    pool.wait_ge(w2_ld, 16 * v + 16)
                    pool.wait_ge(hb_done, n0 * BL + 1)
                    nc.gpsimd.tensor_tensor(tick[:, 1:2], tick[:, 0:1], tick[:, 0:1], ALU.add)
                    for m in range(M1):
                        nc.gpsimd.tensor_copy(w2_hi[:, m], w2_raw[:, m]).then_inc(w2h_ok, 1)
                    pool.wait_ge(w3_ld, 16 * v + 16)
                    pool.wait_ge(y_done, n0 * HALVES + 1)
                    nc.gpsimd.tensor_tensor(tick[:, 2:3], tick[:, 0:1], tick[:, 0:1], ALU.add)
                    nc.gpsimd.tensor_copy(w3_hi[:], w3_raw[:]).then_inc(w3h_ok, 1)
                pool.wait_ge(y_used, HALVES * s + HALVES + 2)
                pool.dma_start(ys[bass.ds(s * SLOT, SLOT), :].rearrange("(t p) d -> p t d", p=P), yo[:]).then_inc(y_st, 16)

            nc.gpsimd.memset(tick[:], 0.0).then_inc(tick_ok, 1)
            pool.wait_ge(tick_ok, 1)
            pool.dma_start(ys[SLOTS0 * SLOT:(SLOTS0 + 1) * SLOT, :].rearrange("(t p) d -> p t d", p=P), k["x"][:, 0:HALVES, :]).then_inc(y_st, 16)
            pool.dma_start(xg[:], xs[0:SLOT, :].rearrange("(t p) d -> p t d", p=P)).then_inc(xg_ld, 16)
            with pool.Fori(0, E0) as e:
                n0, n1, v = slots_of(pool, meta, e, SLOTS0)
                with pool.If(n0 < n1):
                    slot(n0, v, n0)
                    with pool.If(n0 + 1 < n1):
                        with pool.Fori(n0 + 1, n1) as s:
                            slot(s)
                    pool.end_ifs()
                pool.end_ifs()
            pool.wait_ge(y_st, n1 * 16 + 16)

        @block.scalar
        def _(act):
            def slot(s, e):
                for m in range(BL):
                    act.wait_ge(hb_done, s * BL + m + 2)
                    act.wait_ge(hl_ok, s * BL + m + 1)
                    bias = b1[:, bass.ds(e * M1 + m, 1)] if m < M1 else b2[:, bass.ds(e * M2 + m - M1, 1)]
                    nc.scalar.activation(h32[:, m % 2], ps[:, 2 + m % 2, 0:SLOT], ACT.Gelu, bias=bias).then_inc(gelu_ok, 1)
                    if m == M1 - 1:
                        transposed(s + 1)

            def transposed(s):
                act.wait_ge(gt_done, s + 1)
                nc.scalar.activation(gT_hi[:], ps[:, 0, :].rearrange("p (c n) -> p c n", c=C), ACT.Copy).then_inc(gh_ok, 1)

            act.sem_inc(gelu_ok, 2)
            transposed(0)
            act.wait_ge(b_ld, 48)
            with act.Fori(0, E0) as e:
                n0, n1, v = slots_of(act, meta, e, SLOTS0)
                with act.If(n0 < n1):
                    act.wait_ge(w1_ld, 16 * v + 16)
                    act.wait_ge(hb_done, n0 * BL + 1)
                    nc.scalar.activation(w1_hi[:], w1_raw[:], ACT.Copy).then_inc(w1h_ok, 1)
                    with act.Fori(n0, n1) as s:
                        slot(s, e)
                act.end_ifs()

        @block.vector
        def _(dve):
            def transposed(s):
                dve.wait_ge(gh_ok, s + 1)
                nc.vector.tensor_tensor(gT_lo[:], ps[:, 0, :].rearrange("p (c n) -> p c n", c=C), f32(gT_hi[:]),
                                        ALU.subtract).then_inc(gl_ok, 1)

            def slot(s, e, v=None):
                for m in range(BL):
                    n = s * BL + m
                    dve.wait_ge(gelu_ok, n + 3)
                    nc.vector.tensor_copy(h_hi[:, m], h32[:, m % 2]).then_inc(hh_ok, 1)
                    dve.wait_ge(hh_ok, n + 1)
                    nc.vector.tensor_tensor(h_lo[:, m], h32[:, m % 2], f32(h_hi[:, m]), ALU.subtract).then_inc(hl_ok, 1)
                    if v is not None and m < M1:
                        dve.wait_ge(w2h_ok, v * M1 + m + 1)
                        nc.vector.tensor_tensor(w2_lo[:, m], w2_raw[:, m], f32(w2_hi[:, m]), ALU.subtract).then_inc(w2l_ok, 1)
                    if m == M1 - 1:
                        transposed(s + 1)
                if v is not None:
                    dve.wait_ge(w3h_ok, v + 1)
                    nc.vector.tensor_tensor(w3_lo[:], w3_raw[:], f32(w3_hi[:]), ALU.subtract).then_inc(w3l_ok, 1)
                dve.wait_ge(y_st, 16 * s + 16)
                for t in range(HALVES):
                    dve.wait_ge(y_done, HALVES * s + t + 2)
                    nc.vector.tensor_tensor(yo[:, t], ps[:, 4 + t, 0:D], b3[:, bass.ds(e * D, D)], ALU.add).then_inc(y_used, 1)

            for start, by in ((hl_ok, 2), (y_used, 2), (w1l_ok, 1), (w2l_ok, 1), (w3l_ok, 1)):
                dve.sem_inc(start, by)
            transposed(0)
            dve.wait_ge(b_ld, 48)
            with dve.Fori(0, E0) as e:
                n0, n1, v = slots_of(dve, meta, e, SLOTS0)
                with dve.If(n0 < n1):
                    dve.wait_ge(w1h_ok, v + 1)
                    nc.vector.tensor_tensor(w1_lo[:], w1_raw[:], f32(w1_hi[:]), ALU.subtract).then_inc(w1l_ok, 1)
                    slot(n0, e, v)
                    with dve.If(n0 + 1 < n1):
                        with dve.Fori(n0 + 1, n1) as s:
                            slot(s, e)
                    dve.end_ifs()
                dve.end_ifs()

        @block.tensor
        def _(pe):
            def transpose_slot(s):
                pe.wait_ge(xg_ld, 16 * s + 16)
                for c in range(C):
                    for t in range(HALVES):
                        last = nc.tensor.transpose(ps[:, 0, c * SLOT + t * P:c * SLOT + (t + 1) * P],
                                                   xg[:, t, c * P:(c + 1) * P], k["ident"][:])
                last.then_inc(gt_done, 1)

            def slot(s, v=None):
                pe.wait_ge(gl_ok, s + 1)
                if v is not None:
                    pe.wait_ge(w1l_ok, v + 2)
                for m in range(M1):
                    pe.wait_ge(gelu_ok, s * BL + m + 1)
                    w = slice(m * P, (m + 1) * P)
                    for c in range(C):
                        last = mm3(nc, ps[:, 2 + m % 2, 0:SLOT], w1_hi[:, c, w], w1_lo[:, c, w], gT_hi[:, c], gT_lo[:, c], c == 0, c == C - 1)
                    last.then_inc(hb_done, 1)
                transpose_slot(s + 1)
                for m in range(M2):
                    pe.wait_ge(gelu_ok, s * BL + M1 + m + 1)
                    w = slice(m * P, (m + 1) * P)
                    for j in range(M1):
                        if m == 0:
                            pe.wait_ge(hl_ok, s * BL + j + 3)
                            if v is not None:
                                pe.wait_ge(w2l_ok, v * M1 + j + 2)
                        last = mm3(nc, ps[:, 2 + m % 2, 0:SLOT], w2_hi[:, j, w], w2_lo[:, j, w], h_hi[:, j], h_lo[:, j], j == 0, j == M1 - 1)
                    last.then_inc(hb_done, 1)
                if v is not None:
                    pe.wait_ge(w3l_ok, v + 2)
                for t in range(HALVES):
                    pe.wait_ge(y_used, HALVES * s + t + 1)
                    r = slice(t * P, (t + 1) * P)
                    for j in range(M2):
                        if t == 0:
                            pe.wait_ge(hl_ok, s * BL + M1 + j + 3)
                        last = mm3(nc, ps[:, 4 + t, 0:D], h_hi[:, M1 + j, r], h_lo[:, M1 + j, r], w3_hi[:, j], w3_lo[:, j], j == 0, j == M2 - 1)
                    last.then_inc(y_done, 1)

            pe.sem_inc(hb_done, 1)
            pe.sem_inc(y_done, 1)
            transpose_slot(0)
            with pe.Fori(0, E0) as e:
                n0, n1, v = slots_of(pe, meta, e, SLOTS0)
                with pe.If(n0 < n1):
                    slot(n0, v)
                    with pe.If(n0 + 1 < n1):
                        with pe.Fori(n0 + 1, n1) as s:
                            slot(s)
                    pe.end_ifs()
                pe.end_ifs()


def combine_phase(nc, k, L, out=None):
    ctx = ExitStack()
    with ctx:
        yg = ctx.enter_context(nc.sbuf_tensor(f"yg_{L}", [P, NT, D], F32))
        got = [ctx.enter_context(nc.semaphore(f"got{b}_{L}")) for b in range(B)]
        x_ok = ctx.enter_context(nc.semaphore(f"x_ok_{L}"))
        o_st = ctx.enter_context(nc.semaphore(f"o_st_{L}"))
        pos, ys = k[f"pos{L}"], k[f"ys{L}"]
        block = ctx.enter_context(nc.Block())

        @block.gpsimd
        def _(pool):
            for t in range(NT):
                pool.indirect_dma_start(out=yg[:, t, :], out_offset=None, in_=ys,
                                        in_offset=bass.IndirectOffsetOnAxis(ap=pos[:, t:t + 1], axis=0)).then_inc(got[t // TB], 16)

        @block.vector
        def _(dve):
            for t in range(NT):
                if t % TB == 0:
                    dve.wait_ge(got[t // TB], 16 * TB)
                nc.vector.scalar_tensor_tensor(out=k["x"][:, t, :], in0=yg[:, t, :], scalar=k["tg"][:, 2 + L:3 + L],
                                               in1=k["x"][:, t, :], op0=ALU.mult, op1=ALU.add).then_inc(x_ok, 1)

        if out is not None:
            @block.sync
            def _(sp):
                for b in range(B):
                    sp.wait_ge(x_ok, (b + 1) * TB)
                    sp.dma_start(out[b], k["x"][:, b * TB:(b + 1) * TB, :]).then_inc(o_st, 16)
                sp.wait_ge(o_st, 16 * B)


def last_ffn_phase(nc, k, io):
    FF = E1 + 1
    UNITS = T // SLOT
    ctx = ExitStack()
    with ctx:
        def sb(name, shape, dt=F32):
            return ctx.enter_context(nc.sbuf_tensor(f"f_{name}", shape, dt))

        def sem(name):
            return ctx.enter_context(nc.semaphore(f"f_{name}"))

        xn = k["xn"][:].rearrange("p t d -> p (t d)")
        raw = xn[:, 0:C * FH]
        rb_w = xn[:, C * FH:C * FH + MH * P].rearrange("p (m n) -> p m n", m=MH)
        xg = xn[:, 12 * D:14 * D].rearrange("p (t d) -> p t d", t=HALVES)
        yo = xn[:, 14 * D:16 * D].rearrange("p (t d) -> p t d", t=HALVES)
        w1_hi, w1_lo = sb("w1_hi", [P, FF, C, FH], F32R), sb("w1_lo", [P, FF, C, FH], F32R)
        w2_hi, w2_lo = sb("w2_hi", [P, FF, MH, D], F32R), sb("w2_lo", [P, FF, MH, D], F32R)
        b1, b2 = sb("b1", [P, FF * MH]), sb("b2", [P, FF, D])
        rb = sb("rb", [P, E1 * MH])
        rb_hi, rb_lo = sb("rb_hi", [P, MH, P], F32R), sb("rb_lo", [P, MH, P], F32R)
        row = sb("row", [P, E1, D])
        gT_hi, gT_lo = sb("gT_hi", [P, C, SLOT], F32R), sb("gT_lo", [P, C, SLOT], F32R)
        h32 = sb("h32", [P, 2, SLOT])
        h_hi, h_lo = sb("h_hi", [P, MH, SLOT], F32R), sb("h_lo", [P, MH, SLOT], F32R)
        chain_s = sem("chain")
        b_ld, w_ld, wh_ok, wl_ok, xg_ld, y_st = (sem(n) for n in ("b_ld", "w_ld", "wh_ok", "wl_ok", "xg_ld", "y_st"))
        rb_ok, row_done, row_ok = sem("rb_ok"), sem("row_done"), sem("row_ok")
        gt_done, gh_ok, gl_ok, hb_done = (sem(n) for n in ("gt_done", "gh_ok", "gl_ok", "hb_done"))
        relu_ok, hh_ok, hl_ok, y_done, y_used = (sem(n) for n in ("relu_ok", "hh_ok", "hl_ok", "y_done", "y_used"))
        ps, meta, xs, ys = k["ps"], k["meta1"], k["xs1"], k["ys1"]
        ORDER = [(2, 0), (2, 1), (0, 1), (1, 1), (0, 0), (1, 0)]
        block = ctx.enter_context(nc.Block())

        def parts(f, which):
            if which == 0:
                return w1_hi[:, f].rearrange("p c n -> p (c n)"), w1_lo[:, f].rearrange("p c n -> p (c n)")
            return w2_hi[:, f].rearrange("p m n -> p (m n)"), w2_lo[:, f].rearrange("p m n -> p (m n)")

        @block.sync
        def _(sp):
            sp.dma_start(b1[:], io["fb1"]).then_inc(b_ld, 16)
            sp.dma_start(b2[:].rearrange("p f d -> p (f d)"), io["fb2"]).then_inc(b_ld, 16)
            for n, (f, which) in enumerate(ORDER):
                if n:
                    sp.wait_ge(wl_ok, n)
                sp.dma_start(raw, io["fw"][which, f]).then_inc(w_ld, 16)

        @block.gpsimd
        def _(pool):
            def slot(s):
                pool.wait_ge(gt_done, s + 1)
                pool.dma_start(xg, xs[bass.ds((s + 1) * SLOT, SLOT), :].rearrange("(t p) d -> p t d", p=P)).then_inc(xg_ld, 16)
                pool.wait_ge(y_used, HALVES * (s + UNITS) + HALVES + 2)
                pool.dma_start(ys[bass.ds(s * SLOT, SLOT), :].rearrange("(t p) d -> p t d", p=P), yo).then_inc(y_st, 16)

            pool.dma_start(ys[SLOTS1 * SLOT:(SLOTS1 + 1) * SLOT, :].rearrange("(t p) d -> p t d", p=P), f32(k["ctx_hi"][:, 0:1]).rearrange("p c b t n -> p (c b t n)").rearrange("p (t d) -> p t d", t=HALVES)).then_inc(y_st, 16)
            pool.dma_start(xg, xs[0:SLOT, :].rearrange("(t p) d -> p t d", p=P)).then_inc(xg_ld, 16)
            for e in range(E1):
                n0, n1, _ = slots_of(pool, meta, e, SLOTS1)
                with pool.If(n0 < n1):
                    with pool.Fori(n0, n1) as s:
                        slot(s)
                pool.end_ifs()
            pool.wait_ge(y_st, n1 * 16 + 16)

        @block.scalar
        def _(act):
            def hidden(u, f):
                for m in range(MH):
                    act.wait_ge(hb_done, u * MH + m + 1)
                    act.wait_ge(hl_ok, u * MH + m + 1)
                    nc.scalar.activation(h32[:, m % 2], ps[:, 2 + m % 2, 0:SLOT], ACT.Relu,
                                         bias=b1[:, f * MH + m:f * MH + m + 1]).then_inc(relu_ok, 1)

            def transposed(s):
                act.wait_ge(gt_done, s + 1)
                nc.scalar.activation(gT_hi[:], ps[:, 0, :].rearrange("p (c n) -> p c n", c=C), ACT.Copy).then_inc(gh_ok, 1)

            act.sem_inc(relu_ok, 2)
            for n, (f, which) in enumerate(ORDER):
                act.wait_ge(w_ld, 16 * (n + 1))
                nc.scalar.activation(parts(f, which)[0], raw, ACT.Copy).then_inc(wh_ok, 1)
            act.wait_ge(b_ld, 32)
            transposed(0)
            with act.Fori(0, UNITS) as u:
                hidden(u, E1)
            for e in range(E1):
                n0, n1, _ = slots_of(act, meta, e, SLOTS1)
                with act.If(n0 < n1):
                    with act.Fori(n0, n1) as s:
                        hidden(s + UNITS, e)
                        transposed(s + 1)
                act.end_ifs()

        @block.vector
        def _(dve):
            chain = [0]

            def link(ins):
                chain[0] += 1
                ins.then_inc(chain_s, 1)
                dve.wait_ge(chain_s, chain[0])

            def transposed(s):
                dve.wait_ge(gh_ok, s + 1)
                nc.vector.tensor_tensor(gT_lo[:], ps[:, 0, :].rearrange("p (c n) -> p c n", c=C), f32(gT_hi[:]),
                                        ALU.subtract).then_inc(gl_ok, 1)

            def hidden(u):
                for m in range(MH):
                    n = u * MH + m
                    dve.wait_ge(relu_ok, n + 3)
                    nc.vector.tensor_copy(h_hi[:, m], h32[:, m % 2]).then_inc(hh_ok, 1)
                    dve.wait_ge(hh_ok, n + 1)
                    nc.vector.tensor_tensor(h_lo[:, m], h32[:, m % 2], f32(h_hi[:, m]), ALU.subtract).then_inc(hl_ok, 1)

            dve.sem_inc(hl_ok, 2)
            dve.sem_inc(y_used, 2)
            for n, (f, which) in enumerate(ORDER):
                dve.wait_ge(wh_ok, n + 1)
                hi, lo = parts(f, which)
                nc.vector.tensor_tensor(lo, raw, f32(hi), ALU.subtract).then_inc(wl_ok, 1)
            dve.wait_ge(b_ld, 32)
            link(nc.vector.tensor_scalar(rb[:], b1[:, 0:E1 * MH], 0.0, None, ALU.max))
            for e in range(E1):
                link(nc.vector.tensor_copy(rb_w, rb[:, e * MH:(e + 1) * MH, None].to_broadcast([P, MH, P])))
                if e:
                    dve.wait_ge(row_done, e)
                link(nc.vector.tensor_copy(rb_hi[:], rb_w))
                nc.vector.tensor_tensor(rb_lo[:], rb_w, f32(rb_hi[:]), ALU.subtract).then_inc(rb_ok, 1)
                dve.wait_ge(rb_ok, e + 1)
            link(nc.vector.tensor_tensor(row[:, 0], b2[:, 0], b2[:, 1], ALU.add))
            link(nc.vector.tensor_tensor(row[:, 0], row[:, 0], b2[:, E1], ALU.add))
            link(nc.vector.tensor_copy(row[:, 1], row[:, 0]))
            dve.wait_ge(row_done, E1)
            for e in range(E1):
                last = nc.vector.tensor_tensor(row[:, e], row[:, e], ps[:, 7 - e, 0:D], ALU.add)
            last.then_inc(row_ok, 1)
            transposed(0)
            with dve.Fori(0, UNITS) as u:
                hidden(u)
                for t in range(HALVES):
                    dve.wait_ge(y_done, HALVES * u + t + 1)
                    xt = k["x"][:, bass.ds(u * HALVES + t, 1), :].rearrange("p t d -> p (t d)")
                    nc.vector.scalar_tensor_tensor(out=xt, in0=ps[:, 4 + t, 0:D], scalar=k["tg"][:, 3:4], in1=xt,
                                                   op0=ALU.mult, op1=ALU.add).then_inc(y_used, 1)
            dve.wait_ge(row_ok, 1)
            for e in range(E1):
                n0, n1, _ = slots_of(dve, meta, e, SLOTS1)
                with dve.If(n0 < n1):
                    with dve.Fori(n0, n1) as s:
                        hidden(s + UNITS)
                        transposed(s + 1)
                        dve.wait_ge(y_st, 16 * s + 16)
                        for t in range(HALVES):
                            dve.wait_ge(y_done, HALVES * (s + UNITS) + t + 1)
                            nc.vector.tensor_tensor(yo[:, t], ps[:, 4 + t, 0:D], row[:, e], ALU.add).then_inc(y_used, 1)
                dve.end_ifs()

        @block.tensor
        def _(pe):
            def transpose_slot(s):
                pe.wait_ge(xg_ld, 16 * s + 16)
                for c in range(C):
                    for t in range(HALVES):
                        last = nc.tensor.transpose(ps[:, 0, c * SLOT + t * P:c * SLOT + (t + 1) * P],
                                                   xg[:, t, c * P:(c + 1) * P], k["ident"][:])
                last.then_inc(gt_done, 1)

            def unit(u, f, xh, xl, between):
                for m in range(MH):
                    pe.wait_ge(relu_ok, u * MH + m + 1)
                    w = slice(m * P, (m + 1) * P)
                    for c in range(C):
                        last = mm3(nc, ps[:, 2 + m % 2, 0:SLOT], w1_hi[:, f, c, w], w1_lo[:, f, c, w], xh(c), xl(c), c == 0, c == C - 1)
                    last.then_inc(hb_done, 1)
                between()
                for t in range(HALVES):
                    pe.wait_ge(y_used, HALVES * u + t + 1)
                    r = slice(t * P, (t + 1) * P)
                    for j in range(MH):
                        if t == 0:
                            pe.wait_ge(hl_ok, u * MH + j + 3)
                        last = mm3(nc, ps[:, 4 + t, 0:D], h_hi[:, j, r], h_lo[:, j, r], w2_hi[:, f, j], w2_lo[:, f, j], j == 0, j == MH - 1)
                    last.then_inc(y_done, 1)

            transpose_slot(0)
            for e in range(E1):
                pe.wait_ge(wl_ok, 3 + e)
                pe.wait_ge(rb_ok, e + 1)
                for j in range(MH):
                    last = mm3(nc, ps[:, 6 + e, 0:D], rb_hi[:, j], rb_lo[:, j], w2_hi[:, e, j], w2_lo[:, e, j], j == 0, j == MH - 1)
                last.then_inc(row_done, 1)
            with pe.Fori(0, UNITS) as u:
                unit(u, E1, lambda c: k["xT_hi"][:, c, bass.ds(u * SLOT, SLOT)],
                     lambda c: k["xT_lo"][:, c, bass.ds(u * SLOT, SLOT)], lambda: None)
            pe.wait_ge(wl_ok, len(ORDER))
            for e in range(E1):
                n0, n1, _ = slots_of(pe, meta, e, SLOTS1)
                with pe.If(n0 < n1):
                    with pe.Fori(n0, n1) as s:
                        pe.wait_ge(gl_ok, s + 1)
                        unit(s + UNITS, e, lambda c: gT_hi[:, c], lambda c: gT_lo[:, c], lambda: transpose_slot(s + 1))
                pe.end_ifs()


def build(nc, io, out):
    ctx = ExitStack()
    with ctx:
        def sb(name, shape, dt=F32):
            return ctx.enter_context(nc.sbuf_tensor(name, shape, dt))

        k = {
            "ps": ctx.enter_context(nc.psum_tensor("psum", [P, 8, 512], F32)),
            "x": sb("x_res", [P, NT, D]),
            "xn": sb("x_norm", [P, NT, D]),
            "ident": sb("ident", [P, P]),
            "head_rows": sb("head_rows", [P, HPC]),
            "below": sb("below", [P, P], BF16),
            "ones_b": sb("ones_b", [P, P], BF16),
            "den_w": sb("den_w", [P, 2 * HD]),
            "g_raw": sb("g_raw", [P, 4]), "tg": sb("tg", [P, 4]),
            "ctx_hi": sb("ctx_hi", [P, C, B, 2, KEYS], F32R), "ctx_lo": sb("ctx_lo", [P, C, B, 2, KEYS], F32R),
            "lg0": sb("lg0", [P, NT, E0]), "lg1": sb("lg1", [P, NT, E1]),
            "pos0": sb("pos0", [P, NT], I32), "pos1": sb("pos1", [P, NT], I32),
            "meta0": sb("meta0", [1, META], I32), "meta1": sb("meta1", [1, META], I32),
        }
        for L, most in ((0, SLOTS0), (1, SLOTS1)):
            for n in ("xs", "ys"):
                k[f"{n}{L}"] = nc.dram_tensor(f"{n}{L}", ((most + 1) * SLOT, D), F32, kind="Internal").ap()
        for L in range(2):
            with ExitStack() as inner:
                def isb(name, shape, dt=F32):
                    return inner.enter_context(nc.sbuf_tensor(f"{name}_{L}", shape, dt))
                if not L:
                    k["zeros"] = isb("zeros", [P, 1024 // P * D])
                    k["ctx_raw"] = isb("ctx_raw", [P, C, B, KEYS])
                k["xT_hi"], k["xT_lo"] = isb("xT_hi", [P, C, T], F32R), isb("xT_lo", [P, C, T], F32R)
                attention_phase(nc, k, L, io)
                routing_phase(nc, k, L)
                if L:
                    last_ffn_phase(nc, k, io)
            if not L:
                experts_phase(nc, k, io)
            combine_phase(nc, k, L, out if L else None)


def kernel(**inputs):
    import concourse.bacc as bacc
    from concourse.bass_utils import run_bass_kernel_spmd

    a = {n: np.asarray(v) for n, v in inputs.items()}

    def split_rows(w):
        w = w.reshape(*w.shape[:-2], w.shape[-2] // P, P, w.shape[-1])
        return np.ascontiguousarray(np.swapaxes(w, -3, -2))

    def columns(b):
        return np.ascontiguousarray(b.reshape(-1, P).T)

    attn = [[a[f"L0_xattn_{n}"].T for n in ("Wq", "Wk", "Wv", "Wo")],
            [a[f"L1_xattn_{n}_w"] for n in ("Wq", "Wk", "Wv", "Wo")]]
    ffn1 = [*a["L1_ffn_w1"], a["L1_ffn_sw1"]]
    ffn2 = [*a["L1_ffn_w2"], a["L1_ffn_sw2"]]
    arrays = {
        "x": a["x"].reshape(T, D),
        "ctx": split_rows(np.ascontiguousarray(a["ctx_1024"].reshape(B * KEYS, D).T)).reshape(P, C, B, KEYS),
        "wa0": np.ascontiguousarray(np.swapaxes(split_rows(np.stack(attn[0])), 0, 1)),
        "wa1": np.ascontiguousarray(np.swapaxes(split_rows(np.stack(attn[1])), 0, 1)),
        "g": np.concatenate([a["g_xattn"], a["g_ffn"]]).reshape(1, 4),
        "mask": np.ascontiguousarray(np.swapaxes(a["mask_1x1xSxS2_ik0"].reshape(TB, P, KEYS), 0, 1)),
        "rw0": split_rows(a["L0_ffn_Wr"]), "rw1": split_rows(np.ascontiguousarray(a["L1_ffn_gate_w"].T)),
        "br": a["L0_ffn_br"].reshape(1, E0),
        "bq": columns(a["L1_xattn_Wq_b"]), "bk": columns(a["L1_xattn_Wk_b"]),
        "bv": a["L1_xattn_Wv_b"].reshape(1, D), "bo": a["L1_xattn_Wo_b"].reshape(1, D),
        "W1": split_rows(a["L0_ffn_W1"]).reshape(E0 * P, C, F1),
        "W2": split_rows(a["L0_ffn_W2"]).reshape(E0 * P, M1, F2),
        "W3": split_rows(a["L0_ffn_W3"]).reshape(E0 * P, M2, D),
        "b1": columns(a["L0_ffn_b1"]), "b2": columns(a["L0_ffn_b2"]), "b3": a["L0_ffn_b3"].reshape(1, E0 * D),
        "fw": np.stack([split_rows(np.stack(ffn1)).reshape(E1 + 1, P, 2048), split_rows(np.stack(ffn2)).reshape(E1 + 1, P, 2048)]),
        "fb1": columns(np.concatenate([a["L1_ffn_b1"].reshape(-1), a["L1_ffn_sb1"]])),
        "fb2": np.concatenate([a["L1_ffn_b2"].reshape(-1), a["L1_ffn_sb2"]]).reshape(1, (E1 + 1) * D),
    }
    nc = bacc.Bacc("TRN2", target_bir_lowering=False, num_devices=1)
    ap = {n: nc.dram_tensor(f"in_{n}", v.shape, mybir.dt.from_np(v.dtype), kind="ExternalInput").ap() for n, v in arrays.items()}
    out = nc.dram_tensor("out_0", (T, D), F32, kind="ExternalOutput").ap()
    rows = "(b t p) d -> b p t d"
    io = dict(ap)
    io["x"] = ap["x"].rearrange(rows, b=B, p=P)
    io["wa"], io["rw"] = (ap["wa0"], ap["wa1"]), (ap["rw0"], ap["rw1"])
    for n in ("g", "br", "bv", "bo", "b3", "fb2"):
        io[n] = ap[n].to_broadcast([P, ap[n].shape[1]])
    build(nc, io, out.rearrange(rows, b=B, p=P))
    r = run_bass_kernel_spmd(nc, [{f"in_{n}": v for n, v in arrays.items()}], core_ids=[0])
    return r.results[0]["out_0"].reshape(B, S, D)
```

```python
import numpy as np
from contextlib import ExitStack

import concourse.bass as bass
from concourse import mybir

F32 = mybir.dt.float32
F32R = mybir.dt.float32r
BF16 = mybir.dt.bfloat16
I32 = mybir.dt.int32
ALU = mybir.AluOpType
ACT = mybir.ActivationFunctionType
AX = mybir.AxisListType

B, S, D = 4, 512, 256
KEYS = 64
HEADS = 16
HD = D // HEADS
P = 128
T = B * S
NT = T // P
TB = S // P
C = D // P
PAIRS = HEADS // 2
HPC = HEADS // C
E0, F1, F2 = 8, 1024, 512
E1, FH = 2, 1024
M1, M2, MH = F1 // P, F2 // P, FH // P
SLOT = 256
HALVES = SLOT // P
SLOTS0 = T // SLOT + E0 - 1
SLOTS1 = T // SLOT + E1 - 1
EPS = 1e-5
MASKED = -1e9 * HD ** 0.5
SCALE = HD ** -0.5
HUGE = 3e38
RSQRT_SEED = 0x5F3759DF
BITS = 4


def f32(ap):
    return ap.bitcast(F32)


def mm3(nc, out, wh, wl, xh, xl, start, stop):
    nc.tensor.matmul(out, wh, xh, start=start, stop=False)
    nc.tensor.matmul(out, wh, xl, start=False, stop=False)
    return nc.tensor.matmul(out, wl, xh, start=False, stop=stop)


def layernorm_stats(nc, link, x_tiles, st, mv, var, half, tmp, rstd, shift):
    n = len(x_tiles)
    for i, x in enumerate(x_tiles):
        last = nc.vector.bn_stats(st[:, i, :], x)
    link(last)
    for i in range(n):
        last = nc.vector.bn_aggr(mv[:, i, :], st[:, i, :])
    link(last)
    link(nc.vector.tensor_scalar(var, mv[:, :, 1], EPS, None, ALU.add))
    nc.vector.tensor_scalar(half, mv[:, :, 1], EPS, -0.5, ALU.add, ALU.mult)
    link(nc.vector.tensor_scalar(rstd.bitcast(I32), var.bitcast(I32), 1, None, ALU.logical_shift_right))
    link(nc.vector.tensor_scalar(rstd.bitcast(I32), rstd.bitcast(I32), -1.0, float(RSQRT_SEED), ALU.mult, ALU.add))
    for _ in range(3):
        link(nc.vector.tensor_tensor(tmp, rstd, rstd, ALU.mult))
        link(nc.vector.tensor_tensor(tmp, tmp, half, ALU.mult))
        link(nc.vector.scalar_tensor_tensor(out=rstd, in0=tmp, scalar=1.5, in1=rstd, op0=ALU.add, op1=ALU.mult))
    return nc.vector.scalar_tensor_tensor(out=shift, in0=mv[:, :, 0], scalar=-1.0, in1=rstd, op0=ALU.mult, op1=ALU.mult)


def attention_phase(nc, k, L, io):
    soft = L == 1
    E = E1 if soft else E0
    ctx = ExitStack()
    with ctx:
        def sb(name, shape, dt=F32):
            return ctx.enter_context(nc.sbuf_tensor(f"{name}_{L}", shape, dt))

        def sem(name):
            return ctx.enter_context(nc.semaphore(f"{name}_{L}"))

        w_raw, ctx_raw = k["w_raw"], k["ctx_raw"]
        w_hi = sb("w_hi", [P, 4, C, D], F32R)
        w_lo = sb("w_lo", [P, 4, C, D], F32R)
        kT = sb("kT", [P, C, B * KEYS])
        kz_hi = sb("kz_hi", [P, B, C, HPC * KEYS], F32R)
        kz_lo = sb("kz_lo", [P, B, C, HPC * KEYS], F32R)
        vz = sb("vz", [P, B, PAIRS, 2 * HD])
        ln_st = sb("ln_st", [P, TB, 6])
        ln_mv = sb("ln_mv", [P, TB, 2])
        ln_var, ln_half, ln_tmp = (sb(n, [P, TB]) for n in ("ln_var", "ln_half", "ln_tmp"))
        ln_rstd, ln_shift = sb("ln_rstd", [P, 2, TB]), sb("ln_shift", [P, 2, TB])
        xq = sb("xq", [P, TB, D])
        qT_hi = sb("qT_hi", [P, 2, C, S], F32R)
        qT_lo = sb("qT_lo", [P, 2, C, S], F32R)
        oT_hi = sb("oT_hi", [P, C, S], F32R)
        oT_lo = sb("oT_lo", [P, C, S], F32R)
        rw = sb("rw", [P, C, E])
        xrT = sb("xrT", [P, C, S]) if not soft else None
        ctx_hi, ctx_lo = (sb(n, [P, C, B, 2, KEYS], F32R) for n in ("ctx_hi", "ctx_lo"))
        if soft:
            bq = sb("bq", [P, C])
            bk = sb("bk", [P, C])
            bv = sb("bv", [P, D])
            bo = sb("bo", [P, D])
            bo_hi = sb("bo_hi", [P, D], F32R)
            bo_lo = sb("bo_lo", [P, D], F32R)
            ones_r = sb("ones_r", [P, P], F32R)
            rw_hi = sb("rw_hi", [P, C, E], F32R)
            rw_lo = sb("rw_lo", [P, C, E], F32R)
            mask_i = sb("mask_i", [P, TB, KEYS], I32)
            cap = sb("cap", [P, TB, KEYS])
            sc = sb("sc", [P, 3, HEADS, KEYS])
            top = sb("top", [P, 2, HEADS])
            pT = sb("pT", [P, PAIRS, S])
            den, rden = sb("den", [P, 2, HEADS]), sb("rden", [P, 2, HEADS])
            yg = sb("yg", [P, TB, D])
        else:
            br = sb("br", [P, E])
            prob = sb("prob", [P, 3, S])

        dve_chain = sem("dve_chain")
        c_ld, ctxh_ok, ctxl_ok = sem("c_ld"), sem("ctxh_ok"), sem("ctxl_ok")
        wh_ok, wl_ok, kp_done, kT_ok, kzh_ok, kzl_ok = (sem(n) for n in ("wh_ok", "wl_ok", "kp_done", "kT_ok", "kzh_ok", "kzl_ok"))
        vp_done, vz_ok, vz0 = sem("vp_done"), sem("vz_ok"), sem("vz0")
        n1_ok, t1_done, th1_ok, tl1_ok = (sem(n) for n in ("n1_ok", "t1_done", "th1_ok", "tl1_ok"))
        n2_ok, t2_done, th2_ok, st1_ok, st2_ok = (sem(n) for n in ("n2_ok", "t2_done", "th2_ok", "st1_ok", "st2_ok"))
        q_done, qh_ok, ql_ok = sem("q_done"), sem("qh_ok"), sem("ql_ok")
        s_done, p_ok, pv_done, ol_ok = (sem(n) for n in ("s_done", "p_ok", "pv_done", "ol_ok"))
        y_done, y_used, lg_done, lg_ok = (sem(n) for n in ("y_done", "y_used", "lg_done", "lg_ok"))
        if soft:
            cl_ok, mx_ok, sub_ok, sum_ok, nm_ok, pt_done, pc_ok, oh_ok, rw_ok, tl2_ok, yg_ok = (
                sem(n) for n in ("cl_ok", "mx_ok", "sub_ok", "sum_ok", "nm_ok", "pt_done", "pc_ok", "oh_ok", "rw_ok", "tl2_ok", "yg_ok"))
        else:
            x_ld = [sem(f"x_ld{b}") for b in range(B - 1)]
            x_ld.append(x_ld[-1])
            i_ok, mk_ok, tg_ok, g_ld, z_ok, z_st = (sem(n) for n in ("i_ok", "mk_ok", "tg_ok", "g_ld", "z_ok", "z_st"))
        WK, WV, WQ, WO = range(4)
        ps = k["ps"]
        CLD = 16 * (6 if soft else 2)
        TICKS = NT + 2 * TB + 3

        block = ctx.enter_context(nc.Block())

        @block.sync
        def _(sp):
            if not soft:
                sp.dma_start(k["x"][:, 0:TB, :], io["x"][0]).then_inc(x_ld[0], 16)
                sp.dma_start(ctx_raw[:], io["ctx"]).then_inc(k["ctx_ld"], 16)
                sp.dma_start(w_raw[:], io["wa"][L]).then_inc(k["wa_ld"], 16)
                for b in range(1, B):
                    sp.dma_start(k["x"][:, b * TB:(b + 1) * TB, :], io["x"][b]).then_inc(x_ld[b], 16)
                sp.dma_start(k["g_raw"][:], io["g"]).then_inc(g_ld, 16)
                sp.dma_start(br[:], io["br"]).then_inc(c_ld, 16)
                sp.dma_start(rw[:], io["rw"][L]).then_inc(c_ld, 16)
                sp.wait_ge(z_ok, 1)
                sp.wait_ge(x_ld[B - 1], 32)
                nz = 0
                for scratch in ("xs0", "ys0", "xs1", "ys1"):
                    rows = k[scratch].shape[0]
                    for a in range(0, rows, 1024):
                        n = min(1024, rows - a)
                        sp.dma_start(k[scratch][a:a + n, :].rearrange("(p r) d -> p (r d)", p=P),
                                     k["zeros"][:, 0:n // P * D]).then_inc(z_st, 16)
                        nz += 16
                sp.wait_ge(z_st, nz)
            else:
                sp.wait_ge(vz0, 1)
                sp.dma_start(bo[0:1, :], io["bo"]).then_inc(c_ld, 16)
                for dst, src in ((bq, "bq"), (bk, "bk"), (bv, "bv"), (mask_i, "mask")):
                    sp.dma_start(dst[:], io[src]).then_inc(c_ld, 16)
                sp.dma_start(rw[:], io["rw"][L]).then_inc(c_ld, 16)
                sp.wait_ge(wl_ok, 4)
                for h in range(2):
                    sp.dma_start(k["staging"][:, h], io["fw"][0, E1, :, h * FH:(h + 1) * FH]).then_inc(k["fw_ld"][h], 16)

        @block.gpsimd
        def _(pool):
            if soft:
                def gather(b, tiles=range(TB)):
                    if b and 0 in tiles:
                        pool.wait_ge(st1_ok, b)
                    for i in tiles:
                        t = b * TB + i
                        pool.indirect_dma_start(out=yg[:, i, :], out_offset=None, in_=k["ys0"],
                                                in_offset=bass.IndirectOffsetOnAxis(ap=k["pos0"][:, t:t + 1], axis=0)).then_inc(yg_ok, 16)

                nc.gpsimd.memset(bo[:], 0.0).then_inc(vz0, 1)
                nc.gpsimd.memset(vz[:], 0.0).then_inc(vz0, 1)
                for b in range(3):
                    gather(b)
                for n in range(NT + 1):
                    if n < NT:
                        pool.wait_ge(mx_ok, n + 1)
                        nc.gpsimd.tensor_tensor(sc[:, n % 3], sc[:, n % 3], top[:, n % 2, :, None].to_broadcast([P, HEADS, KEYS]),
                                                ALU.subtract).then_inc(sub_ok, 1)
                    if n:
                        pool.wait_ge(sum_ok, n)
                        nc.gpsimd.tensor_tensor(sc[:, (n - 1) % 3], sc[:, (n - 1) % 3],
                                                rden[:, (n - 1) % 2, :, None].to_broadcast([P, HEADS, KEYS]), ALU.mult).then_inc(nm_ok, 1)
                    if n % TB and n // TB + 3 < B:
                        gather(n // TB + 3, (range(0, 2), range(2, 3), range(3, TB))[n % TB - 1])
            else:
                nc.gpsimd.memset(k["ident"][:], 0.0).then_inc(i_ok, 1)
                nc.gpsimd.memset(k["head_rows"][:], 1.0).then_inc(i_ok, 1)
                nc.gpsimd.memset(k["below"][:], 1.0).then_inc(i_ok, 1)
                pool.wait_ge(i_ok, 3)
                nc.gpsimd.affine_select(out=k["ident"][:], in_=k["ident"][:], compare_op=ALU.not_equal, fill=1.0,
                                        base=0, pattern=[[-1, P]], channel_multiplier=1).then_inc(i_ok, 1)
                nc.gpsimd.affine_select(out=k["head_rows"][:], in_=k["head_rows"][:], compare_op=ALU.is_ge, fill=0.0,
                                        base=0, pattern=[[-HD, HPC]], channel_multiplier=1).then_inc(i_ok, 1)
                pool.wait_ge(i_ok, 5)
                nc.gpsimd.affine_select(out=k["head_rows"][:], in_=k["head_rows"][:], compare_op=ALU.is_ge, fill=0.0,
                                        base=HD - 1, pattern=[[HD, HPC]], channel_multiplier=-1).then_inc(mk_ok, 1)
                nc.gpsimd.affine_select(out=k["below"][:], in_=k["below"][:], compare_op=ALU.is_gt, fill=0.0,
                                        base=0, pattern=[[1, P]], channel_multiplier=-1).then_inc(mk_ok, 1)
                nc.gpsimd.memset(k["zeros"][:], 0.0).then_inc(z_ok, 1)
                nc.gpsimd.memset(vz[:], 0.0).then_inc(vz0, 1)
                nc.gpsimd.memset(k["ones_b"][:], 1.0).then_inc(mk_ok, 1)

        @block.scalar
        def _(act):
            act.wait_ge(k["ctx_ld"], 16)
            nc.scalar.activation(ctx_hi[:], ctx_raw[:, :, :, None, :].to_broadcast([P, C, B, 2, KEYS]), ACT.Copy).then_inc(ctxh_ok, 1)
            act.wait_ge(k["wa_ld"], 16 * (L + 1))
            for w in range(4):
                nc.scalar.activation(w_hi[:, w], w_raw[:, w], ACT.Copy).then_inc(wh_ok, 1)
            if not soft:
                act.wait_ge(st1_ok, 1)
                for i in range(TB):
                    last = nc.scalar.activation(xq[:, i, :], k["x"][:, i, :], ACT.Identity,
                                                bias=ln_shift[:, 0, i:i + 1], scale=ln_rstd[:, 0, i:i + 1])
                last.then_inc(n1_ok, 1)
            act.wait_ge(kp_done, 1)
            if soft:
                act.wait_ge(c_ld, CLD)
                for m in range(C):
                    last = nc.scalar.activation(kT[:, m, :], ps[:, 4 + m, 0:B * KEYS], ACT.Identity, bias=bk[:, m:m + 1])
            else:
                last = nc.scalar.activation(kT[:], ps[:, 4:6, 0:B * KEYS], ACT.Copy)
            last.then_inc(kT_ok, 1)
            act.wait_ge(kT_ok, 1)
            if not soft:
                act.wait_ge(mk_ok, 3)

            def spread(c):
                for h in range(HPC):
                    nc.scalar.activation(kz_hi[:, :, c, h * KEYS:(h + 1) * KEYS],
                                         kT[:, c, :].rearrange("p (b n) -> p b n", b=B), ACT.Copy,
                                         scale=k["head_rows"][:, h:h + 1]).then_inc(kzh_ok, 1)

            def input_hi(b):
                act.wait_ge(t1_done, b + 1)
                nc.scalar.activation(k["xT_hi"][:, :, b * S:(b + 1) * S], ps[:, 0:2, :], ACT.Copy).then_inc(th1_ok, 1)

            def q_hi(b):
                act.wait_ge(q_done, b + 1)
                if b >= 2:
                    act.wait_ge(s_done, (TB if soft else PAIRS) * (b - 1))
                if soft:
                    for m in range(C):
                        last = nc.scalar.activation(qT_hi[:, b % 2, m], ps[:, 2 + m, :], ACT.Identity, bias=bq[:, m:m + 1])
                else:
                    last = nc.scalar.activation(qT_hi[:, b % 2], ps[:, 2:4, :], ACT.Copy)
                last.then_inc(qh_ok, 1)

            def norm_1(b):
                act.wait_ge(st1_ok, b + 1)
                if b:
                    act.wait_ge(t1_done, b)
                for i in range(TB):
                    last = nc.scalar.activation(xq[:, i, :], k["x"][:, b * TB + i, :], ACT.Identity,
                                                bias=ln_shift[:, 0, i:i + 1], scale=ln_rstd[:, 0, i:i + 1])
                last.then_inc(n1_ok, 1)

            def norm_2(b):
                act.wait_ge(st2_ok, b + 1)
                for i in range(TB):
                    last = nc.scalar.activation(k["xn"][:, b * TB + i, :], k["x"][:, b * TB + i, :], ACT.Identity,
                                                bias=ln_shift[:, 1, i:i + 1], scale=ln_rstd[:, 1, i:i + 1])
                last.then_inc(n2_ok, 1)

            spread(0)
            if soft:
                norm_1(0)
            input_hi(0)
            spread(1)
            q_hi(0)
            if soft:
                norm_1(1)
                input_hi(1)
            if not soft:
                act.wait_ge(g_ld, 16)
                nc.scalar.activation(k["tg"][:], k["g_raw"][:], ACT.Tanh).then_inc(tg_ok, 1)

                def attend(b, pairs):
                    for j in pairs:
                        n = b * PAIRS + j
                        act.wait_ge(s_done, n + 1)
                        if n >= 3:
                            act.wait_ge(pv_done, n - 2)
                        nc.scalar.activation(prob[:, n % 3, :], ps[:, 4 + n % 2, :], ACT.Sigmoid, scale=SCALE).then_inc(p_ok, 1)

                for s in range(B + 1):
                    if s < B:
                        attend(s, range(0, 2))
                    if s == 0:
                        norm_1(1)
                    if s + 1 < B:
                        input_hi(s + 1)
                    if s < B:
                        attend(s, range(2, 5))
                    if s >= 1:
                        norm_2(s - 1)
                    if s + 1 < B:
                        q_hi(s + 1)
                    if s < B:
                        attend(s, range(5, PAIRS))
                    if s + 2 < B:
                        norm_1(s + 2)
                    if s >= 1:
                        act.wait_ge(t2_done, s)
                        if s > 1:
                            act.wait_ge(lg_done, s - 1)
                        nc.scalar.activation(xrT[:], ps[:, 0:2, :], ACT.Copy).then_inc(th2_ok, 1)
            else:
                for n in range(TICKS):
                    b, r = divmod(n, TB)
                    if r == 1 and b + 1 < B:
                        q_hi(b + 1)
                    if r == 3 and 0 <= b - 1 < B:
                        act.wait_ge(pv_done, b)
                        if b >= 2:
                            act.wait_ge(y_done, b - 1)
                        nc.scalar.activation(oT_hi[:], ps[:, 2:4, :], ACT.Copy).then_inc(oh_ok, 1)
                    if 1 <= n < NT + 1:
                        act.wait_ge(sub_ok, n)
                        nc.scalar.activation(sc[:, (n - 1) % 3], sc[:, (n - 1) % 3], ACT.Exp, scale=SCALE).then_inc(p_ok, 1)
                    if 2 <= n < NT + 2:
                        act.wait_ge(pt_done, n - 1)
                        if (n - 2) % TB == 0 and n > 2:
                            act.wait_ge(pv_done, (n - 2) // TB)
                        i = (n - 2) % TB
                        nc.scalar.activation(pT[:, :, i * P:(i + 1) * P], ps[:, 4:6, :].rearrange("p a (j q) -> p (a j) q", q=P),
                                             ACT.Copy).then_inc(pc_ok, 1)
                    if r == 0 and 0 <= b - 3 < B:
                        act.wait_ge(t2_done, b - 2)
                        nc.scalar.activation(k["xT_hi"][:, :, (b - 3) * S:(b - 2) * S], ps[:, 0:2, :], ACT.Copy).then_inc(th2_ok, 1)
                    if r == 1 and b + 2 < B:
                        norm_1(b + 2)
                    if r == 2 and 0 <= b - 2 < B:
                        norm_2(b - 2)
                    if r == 3 and b + 2 < B:
                        input_hi(b + 2)

        @block.vector
        def _(dve):
            chain = [0]

            def link(ins):
                chain[0] += 1
                ins.then_inc(dve_chain, 1)
                dve.wait_ge(dve_chain, chain[0])

            def statistics(b, kind, done, used):
                if b:
                    dve.wait_ge(used, b)
                layernorm_stats(nc, link, [k["x"][:, t, :] for t in range(b * TB, (b + 1) * TB)], ln_st, ln_mv, ln_var[:],
                                ln_half[:], ln_tmp[:], ln_rstd[:, kind], ln_shift[:, kind]).then_inc(done, 1)
                dve.wait_ge(done, b + 1)

            def norm_1(b):
                if soft:
                    dve.wait_ge(yg_ok, 16 * TB * (b + 1))
                    xb = k["x"][:, b * TB:(b + 1) * TB, :]
                    link(nc.vector.scalar_tensor_tensor(out=xb, in0=yg[:], scalar=k["tg"][:, 2:3], in1=xb, op0=ALU.mult, op1=ALU.add))
                else:
                    dve.wait_ge(x_ld[b], 16 if b < B - 2 else 32)
                statistics(b, 0, st1_ok, n1_ok)

            def norm_2(b):
                statistics(b, 1, st2_ok, n2_ok)

            def input_lo(b, th, tl):
                dve.wait_ge(th, b + 1)
                nc.vector.tensor_tensor(k["xT_lo"][:, :, b * S:(b + 1) * S], ps[:, 0:2, :],
                                        f32(k["xT_hi"][:, :, b * S:(b + 1) * S]), ALU.subtract).then_inc(tl, 1)

            def q_lo(b):
                dve.wait_ge(qh_ok, b + 1)
                if soft:
                    for m in range(C):
                        last = nc.vector.scalar_tensor_tensor(out=qT_lo[:, b % 2, m], in0=ps[:, 2 + m, :], scalar=bq[:, m:m + 1],
                                                              in1=f32(qT_hi[:, b % 2, m]), op0=ALU.add, op1=ALU.subtract)
                else:
                    last = nc.vector.tensor_tensor(qT_lo[:, b % 2], ps[:, 2:4, :], f32(qT_hi[:, b % 2]), ALU.subtract)
                last.then_inc(ql_ok, 1)

            def output_parts(b, c):
                if b and c == 0:
                    dve.wait_ge(y_done, TB * b)
                dve.wait_ge(pv_done, b * PAIRS + (c + 1) * PAIRS // C)
                link(nc.vector.tensor_copy(oT_hi[:, c], ps[:, 6 + c, :]))
                nc.vector.tensor_tensor(oT_lo[:, c], ps[:, 6 + c, :], f32(oT_hi[:, c]), ALU.subtract).then_inc(ol_ok, 1)

            def residual_batch(b):
                dve.wait_ge(y_done, b + 1)
                xb = k["x"][:, b * TB:(b + 1) * TB, :]
                nc.vector.scalar_tensor_tensor(out=xb, in0=ps[:, 0:2, :].rearrange("p a (t d) -> p (a t) d", d=D), scalar=k["tg"][:, L:L + 1],
                                               in1=xb, op0=ALU.mult, op1=ALU.add).then_inc(y_used, 1)
                dve.wait_ge(y_used, b + 1)

            def residual(b):
                if b == 0 and not soft:
                    dve.wait_ge(tg_ok, 1)
                for i in range(TB):
                    n = b * TB + i
                    dve.wait_ge(y_done, n + 1)
                    nc.vector.scalar_tensor_tensor(out=k["x"][:, n, :], in0=ps[:, 2 + n % 2, 0:D], scalar=k["tg"][:, L:L + 1],
                                                   in1=k["x"][:, n, :], op0=ALU.mult, op1=ALU.add).then_inc(y_used, 1)
                dve.wait_ge(y_used, (b + 1) * TB)

            def logits(b):
                dve.wait_ge(lg_done, b + 1)
                lg = ps[:, 0 if soft else 2, 0:TB * E].rearrange("p (i e) -> p i e", e=E)
                if soft:
                    last = nc.vector.tensor_copy(k["lg1"][:, b * TB:(b + 1) * TB, :], lg)
                else:
                    last = nc.vector.tensor_tensor(k["lg0"][:, b * TB:(b + 1) * TB, :], lg, br[:, None, :].to_broadcast([P, TB, E]), ALU.add)
                last.then_inc(lg_ok, 1)

            def weights_lo(w):
                dve.wait_ge(wh_ok, w + 1)
                nc.vector.tensor_tensor(w_lo[:, w], w_raw[:, w], f32(w_hi[:, w]), ALU.subtract).then_inc(wl_ok, 1)

            def spread_lo(c):
                for h in range(HPC):
                    dve.wait_ge(kzh_ok, c * HPC + h + 1)
                    nc.vector.scalar_tensor_tensor(out=kz_lo[:, :, c, h * KEYS:(h + 1) * KEYS],
                                                   in0=kT[:, c, :].rearrange("p (b n) -> p b n", b=B), scalar=k["head_rows"][:, h:h + 1],
                                                   in1=f32(kz_hi[:, :, c, h * KEYS:(h + 1) * KEYS]),
                                                   op0=ALU.mult, op1=ALU.subtract).then_inc(kzl_ok, 1)

            dve.wait_ge(ctxh_ok, 1)
            nc.vector.tensor_tensor(ctx_lo[:].rearrange("p c b t n -> p (c b) t n"),
                                    ctx_raw[:].rearrange("p c b n -> p (c b) n")[:, :, None, :].to_broadcast([P, C * B, 2, KEYS]),
                                    f32(ctx_hi[:].rearrange("p c b t n -> p (c b) t n")), ALU.subtract).then_inc(ctxl_ok, 1)
            weights_lo(WK)
            weights_lo(WV)
            norm_1(0)
            weights_lo(WQ)
            spread_lo(0)
            input_lo(0, th1_ok, tl1_ok)
            weights_lo(WO)
            dve.wait_ge(c_ld, CLD)
            dve.wait_ge(vz0, 2 if soft else 1)
            for b in range(B):
                dve.wait_ge(vp_done, b + 1)
                bank = (6 + b if b < B // 2 else 4 + b - B // 2)
                src = ps[:, bank, 0:D].rearrange("p (j a d) -> p j a d", a=2, d=HD)
                for a in range(2):
                    r = slice(a * KEYS, (a + 1) * KEYS)
                    if soft:
                        last = nc.vector.tensor_tensor(vz[r, b, :, a * HD:(a + 1) * HD], src[r, :, a, :],
                                                       bv[r, :].rearrange("p (j a d) -> p j a d", a=2, d=HD)[:, :, a, :], ALU.add)
                    else:
                        last = nc.vector.tensor_copy(vz[r, b, :, a * HD:(a + 1) * HD], src[r, :, a, :])
                last.then_inc(vz_ok, 1)
            spread_lo(1)
            if soft:
                link(nc.vector.tensor_copy(rw_hi[:], rw[:]))
                link(nc.vector.tensor_copy(bo_hi[:], bo[:]))
                link(nc.vector.memset(cap[:, 0, :], 1.0))
                nc.vector.tensor_tensor(rw_lo[:], rw[:], f32(rw_hi[:]), ALU.subtract).then_inc(rw_ok, 1)
                nc.vector.tensor_tensor(bo_lo[:], bo[:], f32(bo_hi[:]), ALU.subtract).then_inc(rw_ok, 1)
                nc.vector.tensor_copy(ones_r[:].rearrange("p (a n) -> p a n", a=2), cap[:, 0:1, :].to_broadcast([P, 2, KEYS])).then_inc(rw_ok, 1)
                dve.wait_ge(rw_ok, 3)
                link(nc.vector.tensor_scalar(cap[:], mask_i[:], 0.0, HUGE - MASKED, ALU.not_equal, ALU.mult))
                link(nc.vector.tensor_scalar(cap[:], cap[:], MASKED, None, ALU.add))
            q_lo(0)
            norm_1(1)

            if not soft:
                for s in range(B + 1):
                    if s >= 1:
                        norm_2(s - 1)
                    if s + 1 < B:
                        input_lo(s + 1, th1_ok, tl1_ok)
                    if s < B:
                        output_parts(s, 0)
                    if s + 1 < B:
                        q_lo(s + 1)
                    if s + 2 < B:
                        norm_1(s + 2)
                    if s < B:
                        output_parts(s, 1)
                        residual(s)
                    if s >= 1:
                        logits(s - 1)
            else:
                for n in range(TICKS):
                    b, r = divmod(n, TB)
                    if n < NT:
                        dve.wait_ge(s_done, n + 1)
                        if n >= 3:
                            dve.wait_ge(pt_done, n - 2)
                        nc.vector.scalar_tensor_tensor(out=sc[:, n % 3], in0=ps[:, 6:8, :].rearrange("p c (h n) -> p (c h) n", h=HPC), scalar=MASKED,
                                                       in1=cap[:, r, None, :].to_broadcast([P, HEADS, KEYS]),
                                                       op0=ALU.max, op1=ALU.min).then_inc(cl_ok, 1)
                        dve.wait_ge(cl_ok, n + 1)
                        if n >= 2:
                            dve.wait_ge(sub_ok, n - 1)
                        nc.vector.tensor_reduce(top[:, n % 2], sc[:, n % 3], AX.X, ALU.max).then_inc(mx_ok, 1)
                    if 1 <= n < NT + 1:
                        dve.wait_ge(p_ok, n)
                        if n >= 3:
                            dve.wait_ge(nm_ok, n - 2)
                        link(nc.vector.tensor_reduce(den[:, n % 2], sc[:, (n - 1) % 3], AX.X, ALU.add))
                        nc.vector.reciprocal(rden[:, (n - 1) % 2], den[:, n % 2]).then_inc(sum_ok, 1)
                    if n == 0:
                        input_lo(1, th1_ok, tl1_ok)
                    if r == 0:
                        if 0 <= b - 3 < B:
                            input_lo(b - 3, th2_ok, tl2_ok)
                        if b + 2 < B:
                            norm_1(b + 2)
                    if r == 1:
                        if b + 1 < B:
                            q_lo(b + 1)
                        if 0 <= b - 2 < B:
                            residual_batch(b - 2)
                            norm_2(b - 2)
                    if r == 2 and 0 <= b - 3 < B:
                        logits(b - 3)
                    if r == 3:
                        if b + 2 < B:
                            input_lo(b + 2, th1_ok, tl1_ok)
                        if 0 <= b - 1 < B:
                            dve.wait_ge(oh_ok, b)
                            nc.vector.tensor_tensor(oT_lo[:], ps[:, 2:4, :], f32(oT_hi[:]), ALU.subtract).then_inc(ol_ok, 1)

        @block.tensor
        def _(pe):
            def input_T(b):
                pe.wait_ge(n1_ok, b + 1)
                if b:
                    pe.wait_ge(tl1_ok, b)
                if not soft and b >= 3:
                    pe.wait_ge(th2_ok, b - 2)
                for c in range(C):
                    for i in range(TB):
                        last = nc.tensor.transpose(ps[:, c, i * P:(i + 1) * P], xq[:, i, c * P:(c + 1) * P], k["ident"][:])
                last.then_inc(t1_done, 1)

            def q_proj(b):
                pe.wait_ge(tl1_ok, b + 1)
                pe.wait_ge(wl_ok, WQ + 1)
                if b:
                    pe.wait_ge(ql_ok, b)
                if not soft:
                    if b >= 2:
                        pe.wait_ge(y_used, TB * (b - 1))
                    if b >= 3:
                        pe.wait_ge(lg_ok, b - 2)
                elif b >= 3:
                    pe.wait_ge(ol_ok, b - 2)
                for m in range(C):
                    for c in range(C):
                        w = slice(m * P, (m + 1) * P)
                        last = mm3(nc, ps[:, 2 + m, :], w_hi[:, WQ, c, w], w_lo[:, WQ, c, w],
                                   k["xT_hi"][:, c, b * S:(b + 1) * S], k["xT_lo"][:, c, b * S:(b + 1) * S], c == 0, c == C - 1)
                last.then_inc(q_done, 1)

            def project(b):
                pe.wait_ge(ol_ok, (1 if soft else C) * (b + 1))
                pe.wait_ge(wl_ok, 4)
                for i in range(TB):
                    n = b * TB + i
                    if soft:
                        o = ps[:, i // 2, (i % 2) * D:(i % 2 + 1) * D]
                    else:
                        o = ps[:, 2 + n % 2, 0:D]
                        if n >= 2:
                            pe.wait_ge(y_used, n - 1)
                    for c in range(C):
                        t = slice(i * P, (i + 1) * P)
                        last = mm3(nc, o, oT_hi[:, c, t], oT_lo[:, c, t],
                                   w_hi[:, WO, c, :], w_lo[:, WO, c, :], c == 0, c == C - 1 and not soft)
                    if soft:
                        nc.tensor.matmul(o, ones_r[:], bo_hi[:], start=False, stop=False)
                        last = nc.tensor.matmul(o, ones_r[:], bo_lo[:], start=False, stop=True)
                    if not soft or i == TB - 1:
                        last.then_inc(y_done, 1)

            def rows_T(b):
                pe.wait_ge(n2_ok, b + 1)
                for c in range(C):
                    for i in range(TB):
                        last = nc.tensor.transpose(ps[:, c, i * P:(i + 1) * P], k["xn"][:, b * TB + i, c * P:(c + 1) * P], k["ident"][:])
                last.then_inc(t2_done, 1)

            def logits(b):
                pe.wait_ge(tl2_ok if soft else th2_ok, b + 1)
                for i in range(TB):
                    t = slice(b * S + i * P, b * S + (i + 1) * P)
                    for c in range(C):
                        o = ps[:, 0 if soft else 2, i * E:(i + 1) * E]
                        if soft:
                            last = mm3(nc, o, k["xT_hi"][:, c, t], k["xT_lo"][:, c, t], rw_hi[:, c, :], rw_lo[:, c, :], c == 0, c == C - 1)
                        else:
                            last = nc.tensor.matmul(o, xrT[:, c, i * P:(i + 1) * P], rw[:, c, :], start=c == 0, stop=c == C - 1)
                last.then_inc(lg_done, 1)

            def attend(b, pairs):
                for j in pairs:
                    n = b * PAIRS + j
                    if j < PAIRS:
                        if n >= 2:
                            pe.wait_ge(p_ok, n - 1)
                        c, o = j // 4, (j % 4) * P
                        mm3(nc, ps[:, 4 + n % 2, :], kz_hi[:, b, c, o:o + P], kz_lo[:, b, c, o:o + P],
                            qT_hi[:, b % 2, c], qT_lo[:, b % 2, c], True, True).then_inc(s_done, 1)
                    if j:
                        jj = j - 1
                        pe.wait_ge(p_ok, n)
                        if jj % 4 == 0 and b:
                            pe.wait_ge(ol_ok, C * (b - 1) + jj // 4 + 1)
                        r = 2 * HD * (jj % 4)
                        nc.tensor.matmul(ps[r:r + 2 * HD, 6 + jj // 4, :], vz[:, b, jj, :], prob[:, (n - 1) % 3, :],
                                         start=True, stop=True).then_inc(pv_done, 1)

            def scores(n):
                b, i = divmod(n, TB)
                if i == 0:
                    pe.wait_ge(ql_ok, b + 1)
                if n:
                    pe.wait_ge(cl_ok, n)
                t = slice(i * P, (i + 1) * P)
                for c in range(C):
                    last = mm3(nc, ps[:, 6 + c, :], qT_hi[:, b % 2, c, t], qT_lo[:, b % 2, c, t],
                               kz_hi[:, b, c, :], kz_lo[:, b, c, :], True, True)
                last.then_inc(s_done, 1)

            def probs_T(n):
                pe.wait_ge(nm_ok, n + 1)
                if n:
                    pe.wait_ge(pc_ok, n)
                for j in range(PAIRS):
                    last = nc.tensor.transpose(ps[:, 4 + j // 4, (j % 4) * P:(j % 4 + 1) * P],
                                               sc[:, n % 3, 2 * j:2 * j + 2, :].rearrange("p h n -> p (h n)"), k["ident"][:])
                last.then_inc(pt_done, 1)

            def weighted(b):
                pe.wait_ge(pc_ok, TB * (b + 1))
                pe.wait_ge(ql_ok, min(b + 3, B))
                for j in range(PAIRS):
                    r, c = 2 * HD * (j % 4), j // 4
                    last = nc.tensor.matmul(ps[r:r + 2 * HD, 2 + c, :], vz[:, b, j, :], pT[:, j, :], start=True, stop=True)
                last.then_inc(pv_done, 1)

            pe.wait_ge(wl_ok, WK + 1)
            pe.wait_ge(ctxl_ok, 1)
            for m in range(C):
                for c in range(C):
                    w = slice(m * P, (m + 1) * P)
                    last = mm3(nc, ps[:, 4 + m, 0:B * KEYS], w_hi[:, WK, c, w], w_lo[:, WK, c, w],
                               ctx_hi[:, c, :, 0, :], ctx_lo[:, c, :, 0, :], c == 0, c == C - 1)
            last.then_inc(kp_done, 1)
            pe.wait_ge(wl_ok, WV + 1)
            for b in range(B):
                if b == B // 2:
                    pe.wait_ge(kT_ok, 1)
                bank = (6 + b if b < B // 2 else 4 + b - B // 2)
                for c in range(C):
                    last = mm3(nc, ps[:, bank, 0:D], ctx_hi[:, c, b].rearrange("p t n -> p (t n)"),
                               ctx_lo[:, c, b].rearrange("p t n -> p (t n)"), w_hi[:, WV, c, :], w_lo[:, WV, c, :], c == 0, c == C - 1)
                last.then_inc(vp_done, 1)
            if not soft:
                pe.wait_ge(i_ok, 5)
                pe.wait_ge(mk_ok, 3)
            input_T(0)
            q_proj(0)
            if soft:
                pe.wait_ge(rw_ok, 3)
            pe.wait_ge(c_ld, CLD)
            pe.wait_ge(kT_ok, 1)
            pe.wait_ge(kzl_ok, HEADS)
            pe.wait_ge(vz_ok, B)
            if not soft:
                for s in range(B + 1):
                    if s < B:
                        pe.wait_ge(ql_ok, s + 1)
                        attend(s, range(0, 2))
                    if s + 1 < B:
                        input_T(s + 1)
                    if s < B:
                        attend(s, range(2, 5))
                    if s + 1 < B:
                        q_proj(s + 1)
                    if s < B:
                        attend(s, range(5, PAIRS + 1))
                    if s >= 1:
                        pe.wait_ge(tl1_ok, min(s + 2, B))
                        if s >= 2:
                            pe.wait_ge(th2_ok, s - 1)
                        rows_T(s - 1)
                    if s < B:
                        pe.wait_ge(ql_ok, min(s + 2, B))
                        if s >= 2:
                            pe.wait_ge(lg_ok, s - 1)
                        project(s)
                    if s >= 1:
                        pe.wait_ge(y_used, TB * min(s + 1, B))
                        if s >= 2:
                            pe.wait_ge(lg_ok, s - 1)
                        logits(s - 1)
            else:
                scores(0)
                input_T(1)
                for n in range(TICKS):
                    b, r = divmod(n, TB)
                    if r == 2 and 0 <= b - 1 < B:
                        weighted(b - 1)
                    if 2 <= n < NT + 2:
                        probs_T(n - 2)
                    if n + 1 < NT:
                        scores(n + 1)
                    if r == 0:
                        if b + 1 < B:
                            q_proj(b + 1)
                        if 0 <= b - 2 < B:
                            pe.wait_ge(tl1_ok, min(b + 2, B))
                            if b >= 3:
                                pe.wait_ge(tl2_ok, b - 2)
                            project(b - 2)
                    if r == 1 and 0 <= b - 3 < B:
                        pe.wait_ge(y_used, min(b - 1, B))
                        logits(b - 3)
                    if r == 2 and b + 2 < B:
                        if b >= 2:
                            pe.wait_ge(y_used, b - 1)
                        if b >= 3:
                            pe.wait_ge(lg_ok, b - 2)
                        input_T(b + 2)
                    if r == 3 and 0 <= b - 2 < B:
                        pe.wait_ge(tl1_ok, min(b + 3, B))
                        pe.wait_ge(y_used, b - 1)
                        if b >= 3:
                            pe.wait_ge(lg_ok, b - 2)
                        rows_T(b - 2)


class Routing:

    def __init__(self, pool, act, dve, pe, meta_ok, pos_ok):
        self.pool, self.act, self.dve, self.pe = pool, act, dve, pe
        self.meta_ok, self.pos_ok = meta_ok, pos_ok


def routing_steps(nc, k, L, sb, sem):
    E = E1 if L else E0
    lg, pos, meta, xs = (k[f"{n}{L}"] for n in ("lg", "pos", "meta", "xs"))
    top = sb("top", [P, NT])
    eq = sb("eq", [P, NT, E])
    rank = sb("rank", [P, E])
    oh = sb("oh", [P, NT, E])
    oh_b = sb("oh_b", [P, NT, E], BF16)
    tot = sb("tot", [P, E, NT])
    inside = sb("inside", [P, E, NT])
    upto = sb("upto", [P, E, NT])
    step = sb("step", [P, T // SLOT])
    over = sb("over", [P, E, T // SLOT])
    slots = sb("slots", [P, E])
    some = sb("some", [P, E])
    ends = sb("ends", [P, E + 1])
    seen = sb("seen", [P, E + 1])
    ones = sb("ones", [P, E])
    word = sb("word", [P, E])
    place = sb("place", [P, NT, E])
    posf = sb("posf", [P, NT])
    chain_s, consts, oh_ok, pre_ok, pos_ok, scat, meta_ok = (
        sem(n) for n in ("r_chain", "consts", "oh_ok", "pre_ok", "pos_ok", "scat", "meta_ok"))
    if L:
        exp_step = sem("exp_step")
    ps = k["ps"]

    def on_pool(pool, meanwhile):
        for e in range(E):
            nc.gpsimd.memset(rank[:, e:e + 1], float(E - e)).then_inc(consts, 1)
        for j in range(T // SLOT):
            nc.gpsimd.memset(step[:, j:j + 1], float(j * SLOT)).then_inc(consts, 1)
        nc.gpsimd.memset(ones[:], 1.0).then_inc(consts, 1)
        nc.gpsimd.memset(ends[:, 0:1], 0.0).then_inc(consts, 1)
        nc.gpsimd.memset(seen[:, 0:1], 0.0).then_inc(consts, 1)
        nc.gpsimd.memset(meta[:], 0).then_inc(consts, 1)
        nc.gpsimd.memset(inside[:], 1.0).then_inc(consts, 1)
        pool.wait_ge(consts, E + T // SLOT + 5)
        nc.gpsimd.memset(inside[:, :, 0:1], 0.0).then_inc(consts, 1)
        meanwhile()
        pool.wait_ge(pos_ok, 1)
        for t in range(NT):
            pool.indirect_dma_start(out=xs, out_offset=bass.IndirectOffsetOnAxis(ap=pos[:, t:t + 1], axis=0),
                                    in_=k["xn"][:, t, :], in_offset=None).then_inc(scat, 16)
        pool.wait_ge(scat, 16 * NT)

    def on_act(act):
        if L:
            act.wait_ge(exp_step, 1)
            nc.scalar.activation(eq[:], eq[:], ACT.Exp).then_inc(exp_step, 1)

    def on_dve(dve, between=lambda step: None):
        chain = [0]

        def link(ins):
            chain[0] += 1
            ins.then_inc(chain_s, 1)
            dve.wait_ge(chain_s, chain[0])

        def first_best(src):
            link(nc.vector.tensor_reduce(top[:], src, AX.X, ALU.max))
            link(nc.vector.tensor_tensor(eq[:], src, top[:, :, None].to_broadcast([P, NT, E]), ALU.is_ge))
            link(nc.vector.tensor_tensor(eq[:], eq[:], rank[:, None, :].to_broadcast([P, NT, E]), ALU.mult))
            link(nc.vector.tensor_reduce(top[:], eq[:], AX.X, ALU.max))
            link(nc.vector.tensor_tensor(oh[:], eq[:], top[:, :, None].to_broadcast([P, NT, E]), ALU.is_ge))

        dve.wait_ge(consts, E + T // SLOT + 6)
        if L:
            link(nc.vector.tensor_reduce(top[:], lg[:], AX.X, ALU.max))
            nc.vector.tensor_tensor(eq[:], lg[:], top[:, :, None].to_broadcast([P, NT, E]), ALU.subtract).then_inc(exp_step, 1)
            dve.wait_ge(exp_step, 2)
            link(nc.vector.tensor_copy(lg[:], eq[:]))
        first_best(lg[:])
        nc.vector.tensor_copy(oh_b[:], oh[:]).then_inc(oh_ok, 1)
        between(0)
        dve.wait_ge(pre_ok, 1)
        link(nc.vector.tensor_copy(tot[:], ps[:, 1, 0:NT * E].rearrange("p (t e) -> p e t", e=E)))
        link(nc.vector.tensor_tensor_scan(upto[:].rearrange("p e t -> p (e t)"), inside[:].rearrange("p e t -> p (e t)"),
                                          tot[:].rearrange("p e t -> p (e t)"), 0.0, ALU.mult, ALU.add))
        link(nc.vector.tensor_tensor(over[:], upto[:, :, NT - 1:NT].to_broadcast([P, E, T // SLOT]),
                                     step[:, None, :].to_broadcast([P, E, T // SLOT]), ALU.is_gt))
        link(nc.vector.tensor_reduce(slots[:], over[:], AX.X, ALU.add))
        link(nc.vector.tensor_scalar(some[:], slots[:], 0.0, None, ALU.is_gt))
        link(nc.vector.tensor_tensor_scan(ends[:, 1:E + 1], ones[:], slots[:], 0.0, ALU.mult, ALU.add))
        link(nc.vector.tensor_tensor_scan(seen[:, 1:E + 1], ones[:], some[:], 0.0, ALU.mult, ALU.add))
        link(nc.vector.scalar_tensor_tensor(out=word[:], in0=ends[:, 1:E + 1], scalar=float(1 << BITS), in1=ends[:, 0:E],
                                            op0=ALU.mult, op1=ALU.add))
        link(nc.vector.scalar_tensor_tensor(out=word[:], in0=seen[:, 0:E], scalar=float(1 << 2 * BITS), in1=word[:],
                                            op0=ALU.mult, op1=ALU.add))
        nc.vector.tensor_copy(meta[0:1, 0:E], word[0:1, :]).then_inc(meta_ok, 1)
        nc.vector.tensor_copy(meta[0:1, E:E + 1], seen[0:1, E:E + 1]).then_inc(meta_ok, 1)
        between(1)
        link(nc.vector.tensor_tensor(tot[:], upto[:], tot[:], ALU.subtract))
        link(nc.vector.tensor_scalar(slots[:], ends[:, 0:E], float(SLOT), float(0 if L else SLOT), ALU.mult, ALU.add))
        link(nc.vector.tensor_tensor(tot[:], tot[:], slots[:, :, None].to_broadcast([P, E, NT]), ALU.add))
        link(nc.vector.tensor_tensor(place[:], ps[:, 0, 0:NT * E].rearrange("p (t e) -> p t e", e=E),
                                     tot[:].rearrange("p e t -> p t e"), ALU.add))
        link(nc.vector.tensor_tensor(place[:], place[:], oh[:], ALU.mult))
        link(nc.vector.tensor_reduce(posf[:], place[:], AX.X, ALU.add))
        nc.vector.tensor_copy(pos[:], posf[:]).then_inc(pos_ok, 1)

    def on_pe(pe):
        pe.wait_ge(oh_ok, 1)
        rows = oh_b[:].rearrange("p t e -> p (t e)")
        nc.tensor.matmul(ps[:, 0, 0:NT * E], k["below"][:], rows, start=True, stop=True)
        nc.tensor.matmul(ps[:, 1, 0:NT * E], k["ones_b"][:], rows, start=True, stop=True).then_inc(pre_ok, 1)

    return Routing(on_pool, on_act, on_dve, on_pe, meta_ok, pos_ok)


def slots_of(nc, eng, meta, e, most):
    word = eng.value_load(meta[0:1, bass.ds(e, 1)], min_val=0, max_val=(((E0 << BITS) + most) << BITS) + most)
    why = "the table is built with these bounds"
    n0 = nc.s_assert_within(eng.snap(word & ((1 << BITS) - 1)), 0, most - 1, skip_runtime_bounds_check_because=why)
    n1 = nc.s_assert_within(eng.snap((word >> BITS) & ((1 << BITS) - 1)), 0, most, skip_runtime_bounds_check_because=why)
    v = nc.s_assert_within(eng.snap(word >> 2 * BITS), 0, E0, skip_runtime_bounds_check_because=why)
    return n0, n1, v


def experts_phase(nc, k, io):
    BL = M1 + M2
    ctx = ExitStack()
    with ctx:
        def sb(name, shape, dt=F32):
            return ctx.enter_context(nc.sbuf_tensor(f"e_{name}", shape, dt))

        def sem(name):
            return ctx.enter_context(nc.semaphore(f"e_{name}"))

        w1_raw, w2_raw, w3_raw = sb("w1_raw", [P, M1, C, P]), sb("w2_raw", [P, M2, M1, P]), sb("w3_raw", [P, M2, D])
        w1_hi, w2_hi, w3_hi = sb("w1_hi", [P, M1, C, P], F32R), sb("w2_hi", [P, M2, M1, P], F32R), sb("w3_hi", [P, M2, D], F32R)
        w1_lo, w2_lo, w3_lo = sb("w1_lo", [P, M1, C, P], F32R), sb("w2_lo", [P, M2, M1, P], F32R), sb("w3_lo", [P, M2, D], F32R)
        W1Q = 4
        Q1 = M1 // W1Q
        W2_AT = (5,M1-1,M1,M1+1)
        W3_AT = M1 + 2
        FINISH_AT = M1+1
        w2_ld = [sem(f"w2_ld{h}") for h in range(2)]
        b12, b3e = sb("b12", [P, E0 * BL]), sb("b3e", [P, D])
        b3_ld, zero_ok, w1q_ok = sem("b3_ld"), sem("zero_ok"), sem("w1q_ok")
        warm = sb("warm", [P, 2])
        be = sb("be", [P, BL])
        be_ok = sem("be_ok")
        xg = sb("xg", [P, HALVES, D])
        gT_hi, gT_lo = sb("gT_hi", [P, C, SLOT], F32R), sb("gT_lo", [P, C, SLOT], F32R)
        h32 = sb("h32", [P, 2, SLOT])
        h_hi, h_lo = sb("h_hi", [P, BL, SLOT], F32R), sb("h_lo", [P, BL, SLOT], F32R)
        yo = sb("yo", [P, HALVES, D])
        b_ld, w1_ld, w3_ld, xg_ld, y_st = (sem(n) for n in ("b_ld", "w1_ld", "w3_ld", "xg_ld", "y_st"))
        w1h_ok, w1l_ok, w2h_ok, w2l_ok, w3h_ok, w3l_ok = (sem(n) for n in ("w1h_ok", "w1l_ok", "w2h_ok", "w2l_ok", "w3h_ok", "w3l_ok"))
        gt_done, gh_ok, gl_ok, hb_done = (sem(n) for n in ("gt_done", "gh_ok", "gl_ok", "hb_done"))
        gelu_ok, hh_ok, hl_ok, y_done, y_used = (sem(n) for n in ("gelu_ok", "hh_ok", "hl_ok", "y_done", "y_used"))
        ps, meta, xs, ys = k["ps"], k["meta0"], k["xs0"], k["ys0"]
        route = routing_steps(nc, k, 0, sb, sem)
        block = ctx.enter_context(nc.Block())

        @block.sync
        def _(sp):
            sp.dma_start(b12[:], io["b12"]).then_inc(b_ld, 16)
            sp.wait_ge(route.meta_ok, 2)
            with sp.Fori(0, E0) as e:
                n0, n1, v = slots_of(nc, sp, meta, e, SLOTS0)
                with sp.If(n0 < n1):
                    sp.wait_ge(w1l_ok, v * W1Q + 1)
                    sp.dma_start(w1_raw[:], io["W1"][bass.ds(e * P, P)]).then_inc(w1_ld, 16)
                    for h in range(2):
                        sp.wait_ge(w2l_ok, v * M2 + (h + 1) * M2 // 2)
                        cols = slice(h * M2 // 2, (h + 1) * M2 // 2)
                        sp.dma_start(w2_raw[:, cols], io["W2"][bass.ds(e * P, P), cols]).then_inc(w2_ld[h], 16)
                    sp.wait_ge(w3l_ok, v + 1)
                    sp.dma_start(w3_raw[:], io["W3"][bass.ds(e * P, P)]).then_inc(w3_ld, 16)
                sp.end_ifs()
            sp.dma_start(k["w_raw"][:], io["wa"][1]).then_inc(k["wa_ld"], 16)

        @block.gpsimd
        def _(pool):
            def rows_of(scratch, s):
                return scratch[bass.ds((s + 1) * SLOT, SLOT), :].rearrange("(t p) d -> p t d", p=P)

            def slot(s, e=None):
                pool.wait_ge(gt_done, s + 1)
                pool.dma_start(xg[:], rows_of(xs, s + 1)).then_inc(xg_ld, 16)
                pool.wait_ge(y_used, HALVES * s + HALVES)
                if e is not None:
                    pool.dma_start(b3e[:], io["b3"][:, bass.ds(e * D, D)]).then_inc(b3_ld, 16)
                pool.dma_start(rows_of(ys, s - 1), yo[:]).then_inc(y_st, 16)

            def prepare():
                nc.gpsimd.memset(warm[:], 0.0).then_inc(zero_ok, 1)
                nc.gpsimd.memset(yo[:], 0.0).then_inc(zero_ok, 1)
                pool.dma_start(b3e[:], io["b3"][:, 0:D]).then_inc(b3_ld, 16)

            route.pool(pool, prepare)
            pool.dma_start(xg[:], xs[SLOT:2 * SLOT, :].rearrange("(t p) d -> p t d", p=P)).then_inc(xg_ld, 16)
            pool.wait_ge(zero_ok, 2)
            pool.dma_start(ys[0:SLOT, :].rearrange("(t p) d -> p t d", p=P), yo[:]).then_inc(y_st, 16)
            pool.wait_ge(route.meta_ok, 2)
            with pool.Fori(0, E0) as e:
                n0, n1, v = slots_of(nc, pool, meta, e, SLOTS0)
                with pool.If(n0 < n1):
                    slot(n0, e)
                    with pool.If(n0 + 1 < n1):
                        with pool.Fori(n0 + 1, n1) as s:
                            slot(s)
                    pool.end_ifs()
                pool.end_ifs()
            pool.wait_ge(y_used, HALVES * n1 + HALVES)
            pool.dma_start(rows_of(ys, n1 - 1), yo[:]).then_inc(y_st, 16)
            pool.wait_ge(y_st, n1 * 16 + 32)

        @block.scalar
        def _(act):
            def slot(s, v=None):
                for m in range(BL):
                    act.wait_ge(hb_done, s * BL + m + 2)
                    act.wait_ge(hl_ok, s * BL + m + 1)
                    nc.scalar.activation(h32[:, m % 2], ps[:, 2 + m % 2, 0:SLOT], ACT.Gelu, bias=be[:, m:m + 1]).then_inc(gelu_ok, 1)
                    if v is not None and m in W2_AT:
                        i = W2_AT.index(m)
                        if i % 2 == 0:
                            act.wait_ge(w2_ld[i // 2], 16 * v + 16)
                        nc.scalar.activation(w2_hi[:, i], w2_raw[:, i], ACT.Copy).then_inc(w2h_ok, 1)
                    if v is not None and m == W3_AT:
                        act.wait_ge(w3_ld, 16 * v + 16)
                        act.wait_ge(y_done, (s + 1) * HALVES + 1)
                        nc.scalar.activation(w3_hi[:], w3_raw[:], ACT.Copy).then_inc(w3h_ok, 1)
                    if m == M1 - 1:
                        transposed(s + 1)

            def transposed(s):
                act.wait_ge(gt_done, s + 1)
                nc.scalar.activation(gT_hi[:], ps[:, 0, :].rearrange("p (c n) -> p c n", c=C), ACT.Copy).then_inc(gh_ok, 1)

            act.sem_inc(gelu_ok, 2)
            act.wait_ge(zero_ok, 1)
            act.wait_ge(route.meta_ok, 2)
            with act.Fori(0, E0) as e:
                n0, n1, v = slots_of(nc, act, meta, e, SLOTS0)
                with act.If(n0 < n1):
                    nc.scalar.activation(warm[:, 1:2], warm[:, 0:1], ACT.Gelu)
                    act.wait_ge(w1_ld, 16 * v + 16)
                    act.wait_ge(hb_done, n0 * BL + 1)
                    for h in range(1, W1Q):
                        w = slice(h * Q1, (h + 1) * Q1)
                        nc.scalar.activation(w1_hi[:, w], w1_raw[:, w], ACT.Copy).then_inc(w1h_ok, 1)
                    with act.If(v < 1):
                        transposed(0)
                    act.end_ifs()
                    act.wait_ge(be_ok, v + 1)
                    slot(n0, v)
                    with act.If(n0 + 1 < n1):
                        with act.Fori(n0 + 1, n1) as s:
                            slot(s)
                    act.end_ifs()
                act.end_ifs()

        @block.vector
        def _(dve):
            def transposed(s):
                dve.wait_ge(gh_ok, s + 1)
                nc.vector.tensor_tensor(gT_lo[:], ps[:, 0, :].rearrange("p (c n) -> p c n", c=C), f32(gT_hi[:]),
                                        ALU.subtract).then_inc(gl_ok, 1)

            def finish(s, loads):
                dve.wait_ge(b3_ld, 16 * loads)
                dve.wait_ge(y_st, 16 * s + 16)
                for t in range(HALVES):
                    dve.wait_ge(y_done, HALVES * s + t + 2)
                    nc.vector.tensor_tensor(yo[:, t], ps[:, 4 + t, 0:D], b3e[:], ALU.add).then_inc(y_used, 1)

            def slot(s, v, first):
                for m in range(BL):
                    n = s * BL + m
                    dve.wait_ge(gelu_ok, n + 3)
                    nc.vector.tensor_copy(h_hi[:, m], h32[:, m % 2]).then_inc(hh_ok, 1)
                    dve.wait_ge(hh_ok, n + 1)
                    nc.vector.tensor_tensor(h_lo[:, m], h32[:, m % 2], f32(h_hi[:, m]), ALU.subtract).then_inc(hl_ok, 1)
                    if m == FINISH_AT:
                        finish(s, v + 1 if first else v + 2)
                    if first and m in W2_AT:
                        i = W2_AT.index(m)
                        dve.wait_ge(w2h_ok, v * M2 + i + 1)
                        nc.vector.tensor_tensor(w2_lo[:, i], w2_raw[:, i], f32(w2_hi[:, i]), ALU.subtract).then_inc(w2l_ok, 1)
                    if first and m == W3_AT:
                        dve.wait_ge(w3h_ok, v + 1)
                        nc.vector.tensor_tensor(w3_lo[:], w3_raw[:], f32(w3_hi[:]), ALU.subtract).then_inc(w3l_ok, 1)
                    if m == M1 - 1:
                        transposed(s + 1)

            for start, by in ((hl_ok, 2), (w1l_ok, 1), (w2l_ok, M2), (w3l_ok, 1)):
                dve.sem_inc(start, by)
            route.dve(dve)
            dve.wait_ge(b_ld, 16)
            with dve.Fori(0, E0) as e:
                n0, n1, v = slots_of(nc, dve, meta, e, SLOTS0)
                with dve.If(n0 < n1):
                    dve.wait_ge(gelu_ok, n0 * BL + 2)
                    nc.vector.tensor_copy(be[:], b12[:, bass.ds(e * BL, BL)]).then_inc(be_ok, 1)
                    dve.wait_ge(w1_ld, 16 * v + 16)
                    dve.wait_ge(hb_done, n0 * BL + 1)
                    nc.vector.tensor_copy(w1_hi[:, 0:Q1], w1_raw[:, 0:Q1]).then_inc(w1q_ok, 1)
                    for h in range(W1Q):
                        if h:
                            dve.wait_ge(w1h_ok, (W1Q - 1) * v + h)
                        else:
                            dve.wait_ge(w1q_ok, v + 1)
                        w = slice(h * Q1, (h + 1) * Q1)
                        nc.vector.tensor_tensor(w1_lo[:, w], w1_raw[:, w], f32(w1_hi[:, w]), ALU.subtract).then_inc(w1l_ok, 1)
                    with dve.If(v < 1):
                        transposed(0)
                    dve.end_ifs()
                    slot(n0, v, True)
                    with dve.If(n0 + 1 < n1):
                        with dve.Fori(n0 + 1, n1) as s:
                            slot(s, v, False)
                    dve.end_ifs()
                dve.end_ifs()
            visits = dve.value_load(meta[0:1, E0:E0 + 1], min_val=1, max_val=E0)
            finish(n1, visits + 1)

        @block.tensor
        def _(pe):
            def transpose_slot(s):
                pe.wait_ge(xg_ld, 16 * s + 16)
                for c in range(C):
                    for t in range(HALVES):
                        last = nc.tensor.transpose(ps[:, 0, c * SLOT + t * P:c * SLOT + (t + 1) * P],
                                                   xg[:, t, c * P:(c + 1) * P], k["ident"][:])
                last.then_inc(gt_done, 1)

            def slot(s, v=None):
                pe.wait_ge(gl_ok, s + 1)
                for m in range(M1):
                    if v is not None and m % Q1 == 0:
                        pe.wait_ge(w1l_ok, W1Q * v + m // Q1 + 2)
                    pe.wait_ge(gelu_ok, s * BL + m + 1)
                    for c in range(C):
                        last = mm3(nc, ps[:, 2 + m % 2, 0:SLOT], w1_hi[:, m, c], w1_lo[:, m, c], gT_hi[:, c], gT_lo[:, c], c == 0, c == C - 1)
                    last.then_inc(hb_done, 1)
                transpose_slot(s + 1)
                for m in range(M2):
                    pe.wait_ge(gelu_ok, s * BL + M1 + m + 1)
                    if v is not None:
                        pe.wait_ge(w2l_ok, (v + 1) * M2 + m + 1)
                    for j in range(M1):
                        if m == 0:
                            pe.wait_ge(hl_ok, s * BL + j + 3)
                        last = mm3(nc, ps[:, 2 + m % 2, 0:SLOT], w2_hi[:, m, j], w2_lo[:, m, j], h_hi[:, j], h_lo[:, j], j == 0, j == M1 - 1)
                    last.then_inc(hb_done, 1)
                if v is not None:
                    pe.wait_ge(w3l_ok, v + 2)
                pe.wait_ge(y_used, HALVES * s + 2)
                for j in range(M2):
                    pe.wait_ge(hl_ok, s * BL + M1 + j + 3)
                    for t in range(HALVES):
                        r = slice(t * P, (t + 1) * P)
                        last = mm3(nc, ps[:, 4 + t, 0:D], h_hi[:, M1 + j, r], h_lo[:, M1 + j, r], w3_hi[:, j], w3_lo[:, j], j == 0, j == M2 - 1)
                        if j == M2 - 1:
                            last.then_inc(y_done, 1)

            pe.sem_inc(hb_done, 1)
            pe.sem_inc(y_done, HALVES + 1)
            route.pe(pe)
            pe.wait_ge(route.pos_ok, 1)
            transpose_slot(0)
            pe.wait_ge(route.meta_ok, 2)
            with pe.Fori(0, E0) as e:
                n0, n1, v = slots_of(nc, pe, meta, e, SLOTS0)
                with pe.If(n0 < n1):
                    slot(n0, v)
                    with pe.If(n0 + 1 < n1):
                        with pe.Fori(n0 + 1, n1) as s:
                            slot(s)
                    pe.end_ifs()
                pe.end_ifs()


def last_ffn_phase(nc, k, io, out):
    FF = E1 + 1
    UNITS = T // SLOT
    PB = UNITS // B
    ctx = ExitStack()
    with ctx:
        def sb(name, shape, dt=F32):
            return ctx.enter_context(nc.sbuf_tensor(f"f_{name}", shape, dt))

        def sem(name):
            return ctx.enter_context(nc.semaphore(f"f_{name}"))

        CH = FH
        tick, tick_ok = sb("tick", [P, 2]), sem("tick_ok")
        raw = [k["staging"][:, i] for i in range(2)]
        yg = k["xn"]
        xn = k["xn"][:].rearrange("p t d -> p (t d)")
        xg = xn[:, 12 * D:14 * D].rearrange("p (t d) -> p t d", t=HALVES)
        yo = xn[:, 14 * D:16 * D].rearrange("p (t d) -> p t d", t=HALVES)
        w1_hi, w1_lo = sb("w1_hi", [P, FF, C, FH], F32R), sb("w1_lo", [P, FF, C, FH], F32R)
        w2_hi, w2_lo = sb("w2_hi", [P, FF, MH, D], F32R), sb("w2_lo", [P, FF, MH, D], F32R)
        b1, b2 = sb("b1", [P, FF * MH]), sb("b2", [P, FF, D])
        rb = sb("rb", [P, E1 * MH])
        rb_hi, rb_lo = sb("rb_hi", [P, MH, P], F32R), sb("rb_lo", [P, MH, P], F32R)
        row = k["ctx_raw"][:].rearrange("p c b n -> p (c b n)").rearrange("p (e d) -> p e d", e=E1)
        gT_hi, gT_lo = sb("gT_hi", [P, C, SLOT], F32R), sb("gT_lo", [P, C, SLOT], F32R)
        h32 = sb("h32", [P, 2, SLOT])
        h_hi, h_lo = sb("h_hi", [P, MH, SLOT], F32R), sb("h_lo", [P, MH, SLOT], F32R)
        chain_s = sem("chain")
        b_ld, wh_ok, wl_ok, xg_ld, y_st, got, x_ok, o_st = (
            sem(n) for n in ("b_ld", "wh_ok", "wl_ok", "xg_ld", "y_st", "got", "x_ok", "o_st"))
        w_ld = k["fw_ld"]
        rb_ok, row_done = sem("rb_ok"), sem("row_done")
        gt_done, gh_ok, gl_ok, hb_done = (sem(n) for n in ("gt_done", "gh_ok", "gl_ok", "hb_done"))
        relu_ok, hh_ok, hl_ok, y_done, y_used = (sem(n) for n in ("relu_ok", "hh_ok", "hl_ok", "y_done", "y_used"))
        ps, meta, xs, ys = k["ps"], k["meta1"], k["xs1"], k["ys1"]
        HALF = [(f, which, h) for f, which in ((2, 0), (2, 1), (0, 1), (1, 1), (0, 0), (1, 0)) for h in range(2)]
        EARLY = 4
        route = routing_steps(nc, k, 1, sb, sem)
        block = ctx.enter_context(nc.Block())

        def parts(n):
            f, which, h = HALF[n]
            s = slice(h * CH, (h + 1) * CH)
            if which == 0:
                return [w[:, f].rearrange("p c n -> p (c n)")[:, s] for w in (w1_hi, w1_lo)]
            return [w[:, f].rearrange("p m n -> p (m n)")[:, s] for w in (w2_hi, w2_lo)]

        @block.sync
        def _(sp):
            for n, (f, which, h) in enumerate(HALF):
                if n >= 2:
                    sp.wait_ge(wl_ok, n - 1)
                    sp.dma_start(raw[n % 2], io["fw"][which, f, :, h * CH:(h + 1) * CH]).then_inc(w_ld[n % 2], 16)
                if n == 1:
                    sp.dma_start(b1[:], io["fb1"]).then_inc(b_ld, 16)
                    sp.dma_start(b2[:].rearrange("p f d -> p (f d)"), io["fb2"]).then_inc(b_ld, 16)
            for b in range(B):
                sp.wait_ge(x_ok, (b + 1) * TB)
                sp.dma_start(out[b], k["x"][:, b * TB:(b + 1) * TB, :]).then_inc(o_st, 16)
            sp.wait_ge(o_st, 16 * B)

        @block.gpsimd
        def _(pool):
            def slot(s):
                pool.wait_ge(gt_done, s + 1)
                pool.dma_start(xg, xs[bass.ds((s + 1) * SLOT, SLOT), :].rearrange("(t p) d -> p t d", p=P)).then_inc(xg_ld, 16)
                pool.wait_ge(y_used, HALVES * (s + PB) + HALVES + 2)
                pool.dma_start(ys[bass.ds(s * SLOT, SLOT), :].rearrange("(t p) d -> p t d", p=P), yo).then_inc(y_st, 16)

            route.pool(pool, lambda: nc.gpsimd.memset(tick[:], 0.0).then_inc(tick_ok, 1))
            pool.dma_start(ys[SLOTS1 * SLOT:(SLOTS1 + 1) * SLOT, :].rearrange("(t p) d -> p t d", p=P), yg[:, 0:HALVES, :]).then_inc(y_st, 16)
            pool.dma_start(xg, xs[0:SLOT, :].rearrange("(t p) d -> p t d", p=P)).then_inc(xg_ld, 16)
            pool.wait_ge(route.meta_ok, 2)
            for e in range(E1):
                n0, n1, _ = slots_of(nc, pool, meta, e, SLOTS1)
                with pool.If(n0 < n1):
                    with pool.Fori(n0, n1) as s:
                        slot(s)
                pool.end_ifs()
            pool.wait_ge(y_st, n1 * 16 + 16)
            pool.wait_ge(gt_done, n1 + 1)
            pool.wait_ge(tick_ok, 1)
            nc.gpsimd.tensor_tensor(tick[:, 1:2], tick[:, 0:1], tick[:, 0:1], ALU.add).then_inc(tick_ok, 1)
            pool.wait_ge(tick_ok, 2)
            for t in range(NT):
                pool.indirect_dma_start(out=yg[:, t, :], out_offset=None, in_=ys,
                                        in_offset=bass.IndirectOffsetOnAxis(ap=k["pos1"][:, t:t + 1], axis=0)).then_inc(got, 16)

        @block.scalar
        def _(act):
            def weights_hi(n):
                act.wait_ge(w_ld[n % 2], 16 * (n // 2 + 1))
                nc.scalar.activation(parts(n)[0], raw[n % 2], ACT.Copy).then_inc(wh_ok, 1)

            def hidden(q, f, between=lambda m: None):
                for m in range(MH):
                    act.wait_ge(hb_done, q * MH + m + 1)
                    act.wait_ge(hl_ok, q * MH + m + 1)
                    nc.scalar.activation(h32[:, m % 2], ps[:, 2 + m % 2, 0:SLOT], ACT.Relu,
                                         bias=b1[:, f * MH + m:f * MH + m + 1]).then_inc(relu_ok, 1)
                    between(m)

            def transposed(s):
                act.wait_ge(gt_done, s + 1)
                nc.scalar.activation(gT_hi[:], ps[:, 0, :].rearrange("p (c n) -> p c n", c=C), ACT.Copy).then_inc(gh_ok, 1)

            act.sem_inc(relu_ok, 2)
            weights_hi(0)
            route.act(act)
            for n in range(1, EARLY):
                weights_hi(n)
            act.wait_ge(b_ld, 32)
            for u in range(PB):
                hidden(u, E1, lambda m: weights_hi(EARLY + u * MH // 2 + m // 2) if m % 2 else None)
            transposed(0)
            act.wait_ge(route.meta_ok, 2)
            for e in range(E1):
                n0, n1, _ = slots_of(nc, act, meta, e, SLOTS1)
                with act.If(n0 < n1):
                    with act.Fori(n0, n1) as s:
                        hidden(s + PB, e)
                        transposed(s + 1)
                act.end_ifs()
            with act.Fori(PB, UNITS) as u:
                hidden(u + n1, E1)

        @block.vector
        def _(dve):
            chain = [0]

            def link(ins):
                chain[0] += 1
                ins.then_inc(chain_s, 1)
                dve.wait_ge(chain_s, chain[0])

            def weights_lo(n):
                dve.wait_ge(wh_ok, n + 1)
                hi, lo = parts(n)
                nc.vector.tensor_tensor(lo, raw[n % 2], f32(hi), ALU.subtract).then_inc(wl_ok, 1)

            def transposed(s):
                dve.wait_ge(gh_ok, s + 1)
                nc.vector.tensor_tensor(gT_lo[:], ps[:, 0, :].rearrange("p (c n) -> p c n", c=C), f32(gT_hi[:]),
                                        ALU.subtract).then_inc(gl_ok, 1)

            def hidden(q, between=lambda m: None):
                for m in range(MH):
                    n = q * MH + m
                    dve.wait_ge(relu_ok, n + 3)
                    nc.vector.tensor_copy(h_hi[:, m], h32[:, m % 2]).then_inc(hh_ok, 1)
                    dve.wait_ge(hh_ok, n + 1)
                    nc.vector.tensor_tensor(h_lo[:, m], h32[:, m % 2], f32(h_hi[:, m]), ALU.subtract).then_inc(hl_ok, 1)
                    between(m)

            def constant_hidden(e):
                rb_w = rb[:, e * MH:(e + 1) * MH, None].to_broadcast([P, MH, P])
                link(nc.vector.tensor_copy(rb_hi[:], rb_w))
                nc.vector.tensor_tensor(rb_lo[:], rb_w, f32(rb_hi[:]), ALU.subtract).then_inc(rb_ok, 1)

            def add_shared(q, t, x_tile):
                dve.wait_ge(y_done, HALVES * q + t + 1)
                nc.vector.scalar_tensor_tensor(out=x_tile, in0=ps[:, 4 + t, 0:D], scalar=k["tg"][:, 3:4], in1=x_tile,
                                               op0=ALU.mult, op1=ALU.add).then_inc(y_used, 1)

            def add_routed(t):
                return nc.vector.scalar_tensor_tensor(out=k["x"][:, t, :], in0=yg[:, t, :], scalar=k["tg"][:, 3:4],
                                                      in1=k["x"][:, t, :], op0=ALU.mult, op1=ALU.add)

            dve.sem_inc(hl_ok, 2)
            dve.sem_inc(y_used, 2)
            route.dve(dve, lambda step: weights_lo(step))
            for n in range(2, EARLY):
                weights_lo(n)
            for u in range(PB):
                hidden(u, lambda m: weights_lo(EARLY + u * MH // 2 + m // 2) if m % 2 else None)
                if u == PB - 1:
                    dve.wait_ge(b_ld, 32)
                    link(nc.vector.tensor_scalar(rb[:], b1[:, 0:E1 * MH], 0.0, None, ALU.max))
                    constant_hidden(0)
                for t in range(HALVES):
                    add_shared(u, t, k["x"][:, u * HALVES + t, :])
            for e in range(1, E1):
                dve.wait_ge(row_done, e)
                constant_hidden(e)
            transposed(0)
            link(nc.vector.tensor_tensor(row[:, 0], b2[:, 0], b2[:, 1], ALU.add))
            link(nc.vector.tensor_tensor(row[:, 0], row[:, 0], b2[:, E1], ALU.add))
            link(nc.vector.tensor_copy(row[:, 1], row[:, 0]))
            dve.wait_ge(row_done, E1)
            for e in range(E1):
                link(nc.vector.tensor_tensor(row[:, e], row[:, e], ps[:, 7 - e, 0:D], ALU.add))
            for e in range(E1):
                n0, n1, _ = slots_of(nc, dve, meta, e, SLOTS1)
                with dve.If(n0 < n1):
                    with dve.Fori(n0, n1) as s:
                        hidden(s + PB)
                        transposed(s + 1)
                        dve.wait_ge(y_st, 16 * s + 16)
                        for t in range(HALVES):
                            dve.wait_ge(y_done, HALVES * (s + PB) + t + 1)
                            nc.vector.tensor_tensor(yo[:, t], ps[:, 4 + t, 0:D], row[:, e], ALU.add).then_inc(y_used, 1)
                dve.end_ifs()
            with dve.Fori(PB, UNITS - PB) as u:
                hidden(u + n1)
                for t in range(HALVES):
                    xt = k["x"][:, bass.ds(u * HALVES + t, 1), :].rearrange("p t d -> p (t d)")
                    add_shared(u + n1, t, xt)
            tiles = (B - 1) * TB // PB
            dve.wait_ge(y_used, (UNITS - PB + n1) * HALVES + 2)
            dve.wait_ge(got, 16 * NT)
            for u in range(UNITS - PB, UNITS):
                first = (u - (UNITS - PB)) * tiles
                hidden(u + n1, lambda m: add_routed(first + m).then_inc(x_ok, 1) if m < tiles else None)
                for t in range(HALVES):
                    link(add_routed(u * HALVES + t))
                for t in range(HALVES):
                    add_shared(u + n1, t, k["x"][:, u * HALVES + t, :])
            dve.wait_ge(y_used, (UNITS + n1) * HALVES + 2)
            dve.sem_inc(x_ok, TB)

        @block.tensor
        def _(pe):
            def transpose_slot(s):
                pe.wait_ge(xg_ld, 16 * s + 16)
                for c in range(C):
                    for t in range(HALVES):
                        last = nc.tensor.transpose(ps[:, 0, c * SLOT + t * P:c * SLOT + (t + 1) * P],
                                                   xg[:, t, c * P:(c + 1) * P], k["ident"][:])
                last.then_inc(gt_done, 1)

            def unit(q, f, xh, xl, between=lambda: None, weights=None):
                if weights:
                    pe.wait_ge(wl_ok, weights[0])
                for m in range(MH):
                    pe.wait_ge(relu_ok, q * MH + m + 1)
                    w = slice(m * P, (m + 1) * P)
                    for c in range(C):
                        last = mm3(nc, ps[:, 2 + m % 2, 0:SLOT], w1_hi[:, f, c, w], w1_lo[:, f, c, w], xh(c), xl(c), c == 0, c == C - 1)
                    last.then_inc(hb_done, 1)
                between()
                if weights:
                    pe.wait_ge(wl_ok, weights[1])
                for t in range(HALVES):
                    pe.wait_ge(y_used, HALVES * q + t + 1)
                    r = slice(t * P, (t + 1) * P)
                    for j in range(MH):
                        if t == 0:
                            pe.wait_ge(hl_ok, q * MH + j + 3)
                        last = mm3(nc, ps[:, 4 + t, 0:D], h_hi[:, j, r], h_lo[:, j, r], w2_hi[:, f, j], w2_lo[:, f, j], j == 0, j == MH - 1)
                    last.then_inc(y_done, 1)

            def shared(q, u, weights=None):
                unit(q, E1, lambda c: k["xT_hi"][:, c, bass.ds(u * SLOT, SLOT)],
                     lambda c: k["xT_lo"][:, c, bass.ds(u * SLOT, SLOT)], weights=weights)

            route.pe(pe)
            for u in range(PB):
                shared(u, u, (2, EARLY))
            for e in range(E1):
                pe.wait_ge(wl_ok, EARLY + 2 * (e + 1))
                pe.wait_ge(rb_ok, e + 1)
                for j in range(MH):
                    last = mm3(nc, ps[:, 6 + e, 0:D], rb_hi[:, j], rb_lo[:, j], w2_hi[:, e, j], w2_lo[:, e, j], j == 0, j == MH - 1)
                last.then_inc(row_done, 1)
                if e == 0:
                    pe.wait_ge(route.pos_ok, 1)
                    transpose_slot(0)
            pe.wait_ge(wl_ok, len(HALF))
            pe.wait_ge(route.meta_ok, 2)
            for e in range(E1):
                n0, n1, _ = slots_of(nc, pe, meta, e, SLOTS1)
                with pe.If(n0 < n1):
                    with pe.Fori(n0, n1) as s:
                        pe.wait_ge(gl_ok, s + 1)
                        unit(s + PB, e, lambda c: gT_hi[:, c], lambda c: gT_lo[:, c], lambda: transpose_slot(s + 1))
                pe.end_ifs()
            with pe.Fori(PB, UNITS) as u:
                shared(u + n1, u)


def build(nc, io, out):
    ctx = ExitStack()
    with ctx:
        def sb(name, shape, dt=F32):
            return ctx.enter_context(nc.sbuf_tensor(name, shape, dt))

        k = {
            "ps": ctx.enter_context(nc.psum_tensor("psum", [P, 8, 512], F32)),
            "x": sb("x_res", [P, NT, D]),
            "xn": sb("x_norm", [P, NT, D]),
            "ident": sb("ident", [P, P]),
            "head_rows": sb("head_rows", [P, HPC]),
            "below": sb("below", [P, P], BF16),
            "ones_b": sb("ones_b", [P, P], BF16),
            "w_raw": sb("w_raw", [P, 4, C, D]), "ctx_raw": sb("ctx_raw", [P, C, B, KEYS]),
            "g_raw": sb("g_raw", [P, 4]), "tg": sb("tg", [P, 4]),
            "lg0": sb("lg0", [P, NT, E0]), "lg1": sb("lg1", [P, NT, E1]),
            "pos0": sb("pos0", [P, NT], I32), "pos1": sb("pos1", [P, NT], I32),
            "meta0": sb("meta0", [1, E0 + 1], I32), "meta1": sb("meta1", [1, E1 + 1], I32),
        }
        k["staging"] = k["w_raw"][:].rearrange("p w c d -> p (w c d)").rearrange("p (h n) -> p h n", h=2)
        k["wa_ld"], k["ctx_ld"] = (ctx.enter_context(nc.semaphore(n)) for n in ("wa_ld", "ctx_ld"))
        k["fw_ld"] = [ctx.enter_context(nc.semaphore(f"fw_ld{h}")) for h in range(2)]
        for L, most in ((0, SLOTS0), (1, SLOTS1)):
            for n in ("xs", "ys"):
                k[f"{n}{L}"] = nc.dram_tensor(f"{n}{L}", ((most + 2 - L) * SLOT, D), F32, kind="Internal").ap()
        for L in range(2):
            with ExitStack() as inner:
                def isb(name, shape, dt=F32):
                    return inner.enter_context(nc.sbuf_tensor(f"{name}_{L}", shape, dt))
                if not L:
                    k["zeros"] = isb("zeros", [P, 1024 // P * D])
                k["xT_hi"], k["xT_lo"] = isb("xT_hi", [P, C, T], F32R), isb("xT_lo", [P, C, T], F32R)
                attention_phase(nc, k, L, io)
                if L:
                    last_ffn_phase(nc, k, io, out)
            if not L:
                experts_phase(nc, k, io)


def kernel(**inputs):
    import concourse.bacc as bacc
    from concourse.bass_utils import run_bass_kernel_spmd

    a = {n: np.asarray(v) for n, v in inputs.items()}

    def split_rows(w):
        w = w.reshape(*w.shape[:-2], w.shape[-2] // P, P, w.shape[-1])
        return np.ascontiguousarray(np.swapaxes(w, -3, -2))

    def column_blocks(w):
        w = w.reshape(*w.shape[:-1], w.shape[-1] // P, P)
        return np.ascontiguousarray(np.swapaxes(w, 2, 3))

    def columns(b):
        return np.ascontiguousarray(b.reshape(-1, P).T)

    attn = [[a[f"L0_xattn_{n}"].T for n in ("Wk", "Wv", "Wq", "Wo")],
            [a[f"L1_xattn_{n}_w"] for n in ("Wk", "Wv", "Wq", "Wo")]]
    ffn1 = [*a["L1_ffn_w1"], a["L1_ffn_sw1"]]
    ffn2 = [*a["L1_ffn_w2"], a["L1_ffn_sw2"]]
    arrays = {
        "x": a["x"].reshape(T, D),
        "ctx": split_rows(np.ascontiguousarray(a["ctx_1024"].reshape(B * KEYS, D).T)).reshape(P, C, B, KEYS),
        "wa0": np.ascontiguousarray(np.swapaxes(split_rows(np.stack(attn[0])), 0, 1)),
        "wa1": np.ascontiguousarray(np.swapaxes(split_rows(np.stack(attn[1])), 0, 1)),
        "g": np.concatenate([a["g_xattn"], a["g_ffn"]]).reshape(1, 4),
        "mask": np.ascontiguousarray(np.swapaxes(a["mask_1x1xSxS2_ik0"].reshape(TB, P, KEYS), 0, 1)),
        "rw0": split_rows(a["L0_ffn_Wr"]), "rw1": split_rows(np.ascontiguousarray(a["L1_ffn_gate_w"].T)),
        "br": a["L0_ffn_br"].reshape(1, E0),
        "bq": columns(a["L1_xattn_Wq_b"]), "bk": columns(a["L1_xattn_Wk_b"]),
        "bv": a["L1_xattn_Wv_b"].reshape(1, D), "bo": a["L1_xattn_Wo_b"].reshape(1, D),
        "W1": column_blocks(split_rows(a["L0_ffn_W1"])).reshape(E0 * P, M1, C, P),
        "W2": column_blocks(split_rows(a["L0_ffn_W2"])).reshape(E0 * P, M2, M1, P),
        "W3": split_rows(a["L0_ffn_W3"]).reshape(E0 * P, M2, D),
        "b12": columns(np.concatenate([a["L0_ffn_b1"], a["L0_ffn_b2"]], axis=1)), "b3": a["L0_ffn_b3"].reshape(1, E0 * D),
        "fw": np.stack([split_rows(np.stack(ffn1)).reshape(E1 + 1, P, 2048), split_rows(np.stack(ffn2)).reshape(E1 + 1, P, 2048)]),
        "fb1": columns(np.concatenate([a["L1_ffn_b1"].reshape(-1), a["L1_ffn_sb1"]])),
        "fb2": np.concatenate([a["L1_ffn_b2"].reshape(-1), a["L1_ffn_sb2"]]).reshape(1, (E1 + 1) * D),
    }
    nc = bacc.Bacc("TRN2", target_bir_lowering=False, num_devices=1)
    ap = {n: nc.dram_tensor(f"in_{n}", v.shape, mybir.dt.from_np(v.dtype), kind="ExternalInput").ap() for n, v in arrays.items()}
    out = nc.dram_tensor("out_0", (T, D), F32, kind="ExternalOutput").ap()
    rows = "(b t p) d -> b p t d"
    io = dict(ap)
    io["x"] = ap["x"].rearrange(rows, b=B, p=P)
    io["wa"], io["rw"] = (ap["wa0"], ap["wa1"]), (ap["rw0"], ap["rw1"])
    for n in ("g", "br", "bv", "b3", "fb2"):
        io[n] = ap[n].to_broadcast([P, ap[n].shape[1]])
    build(nc, io, out.rearrange(rows, b=B, p=P))
    r = run_bass_kernel_spmd(nc, [{f"in_{n}": v for n, v in arrays.items()}], core_ids=[0])
    return r.results[0]["out_0"].reshape(B, S, D)
```
